# Optimizing a Trainium2 kernel written in Bass

```python
import numpy as np
import jax
import jax.numpy as jnp

def _softmax(x, axis=-1):
    return jax.nn.softmax(x, axis=axis)

def _gelu(x):
    return jax.nn.gelu(x, approximate=True)

def _silu(x):
    return jax.nn.silu(x)

def _sigmoid(x):
    return jax.nn.sigmoid(x)

def _layernorm(x, axis=-1, eps=1e-05):
    m = jnp.mean(x, axis=axis, keepdims=True)
    v = jnp.var(x, axis=axis, keepdims=True)
    return (x - m) / jnp.sqrt(v + eps)

def _scatter_add(tgt, idx, src, axis=0):
    return tgt.at[idx].add(src)

def _segment_sum(src, seg, n):
    return jax.ops.segment_sum(src, seg, n)
kernel_name = 'mk_vit_tower_d1_tok_img1024_r4_765c38'

def setup_inputs(seed: int=0):
    np.random.seed(seed)
    _w = jnp.asarray

    def _rec_inputs():
        import jax
        import jax.numpy as jnp
        _rk = jax.random.key(seed)
        x = -0.00016672 + 0.999947 * jax.random.normal(jax.random.fold_in(_rk, 1), (16, 3, 96, 96), jnp.float32)
        return x
    x = _rec_inputs()

    def _L0_tok_setup():
        import jax, jax.numpy as jnp
        import numpy as np
        P = 16

        def _patchify(x):
            B, C, H, W = x.shape
            gh, gw = (H // P, W // P)
            x = x.reshape(B, C, gh, P, gw, P)
            x = x.transpose(0, 2, 4, 1, 3, 5)
            return x.reshape(B, gh * gw, C * P * P)
        key = jax.random.key(seed)
        k1, k2, k3, k4, k5 = jax.random.split(key, 5)
        B, C, S = (64, 3, 96)
        lin_in, lout = (P * P * C, 256)
        n_patches = (S // P) ** 2
        return {'x': jax.random.normal(k1, (B, C, S, S), dtype=jnp.float32), 'W': jax.random.normal(k2, (lout, lin_in), dtype=jnp.float32) * 0.02, 'b': jax.random.normal(k3, (lout,), dtype=jnp.float32) * 0.02, 'class_token': jax.random.normal(k4, (1, 1, lout), dtype=jnp.float32) * 0.02, 'pos_embedding': jax.random.normal(k5, (1, n_patches + 1, lout), dtype=jnp.float32) * 0.02}
    _L0_tok_all = _L0_tok_setup()
    _L0_tok_in = {k: v for k, v in _L0_tok_all.items() if k in ('W', 'b', 'class_token', 'pos_embedding')}
    del _L0_tok_all

    def _L0_attn_setup():
        import jax, jax.numpy as jnp
        import numpy as np
        N_HEAD = 16
        Q_DIM = 64
        V_DIM = 64
        WINDOW = 129
        DIL = 1
        key = jax.random.key(seed)
        ks = jax.random.split(key, 9)
        B, N, E = (1, 512, 256)
        s = 0.02
        return {'x': jax.random.normal(ks[0], (B, N, E), jnp.float32), 'Wq': jax.random.normal(ks[1], (E, N_HEAD * Q_DIM), jnp.float32) * s, 'bq': jax.random.normal(ks[2], (N_HEAD * Q_DIM,), jnp.float32) * s, 'Wk': jax.random.normal(ks[3], (E, N_HEAD * Q_DIM), jnp.float32) * s, 'bk': jax.random.normal(ks[4], (N_HEAD * Q_DIM,), jnp.float32) * s, 'Wv': jax.random.normal(ks[5], (E, N_HEAD * V_DIM), jnp.float32) * s, 'bv': jax.random.normal(ks[6], (N_HEAD * V_DIM,), jnp.float32) * s, 'Wo': jax.random.normal(ks[7], (N_HEAD * V_DIM, E), jnp.float32) * s, 'bo': jax.random.normal(ks[8], (E,), jnp.float32) * s}
    _L0_attn_all = _L0_attn_setup()
    _L0_attn_in = {k: v for k, v in _L0_attn_all.items() if k in ('Wq', 'bq', 'Wk', 'bk', 'Wv', 'bv', 'Wo', 'bo')}
    del _L0_attn_all

    def _L0_ffn_setup():
        import math
        import jax, jax.numpy as jnp
        import numpy as np
        D_MODEL = 256
        D_HIDDEN = 1024
        N_EXPERTS = 8
        TOP_K = 2
        CAPACITY_FACTOR = 1.25
        key = jax.random.key(seed)
        ks = jax.random.split(key, 8)
        s = 0.02
        x = jax.random.normal(ks[0], (4, 512, D_MODEL), dtype=jnp.float32)
        router_w = jax.random.normal(ks[1], (D_MODEL, N_EXPERTS), dtype=jnp.float32) * s
        router_b = jnp.zeros((N_EXPERTS,), dtype=jnp.float32)
        w1 = jax.random.normal(ks[2], (N_EXPERTS, D_MODEL, D_HIDDEN), dtype=jnp.float32) * s
        b1 = jnp.zeros((N_EXPERTS, D_HIDDEN), dtype=jnp.float32)
        w2 = jax.random.normal(ks[3], (N_EXPERTS, D_HIDDEN, D_MODEL), dtype=jnp.float32) * s
        b2 = jnp.zeros((N_EXPERTS, D_MODEL), dtype=jnp.float32)
        return {'x': x, 'router_w': router_w, 'router_b': router_b, 'w1': w1, 'b1': b1, 'w2': w2, 'b2': b2}
    _L0_ffn_all = _L0_ffn_setup()
    _L0_ffn_in = {k: v for k, v in _L0_ffn_all.items() if k in ('router_w', 'router_b', 'w1', 'b1', 'w2', 'b2')}
    del _L0_ffn_all
    return {'x': x, 'L0_tok_W': _L0_tok_in['W'], 'L0_tok_b': _L0_tok_in['b'], 'L0_tok_class_token': _L0_tok_in['class_token'], 'L0_tok_pos_embedding': _L0_tok_in['pos_embedding'], 'L0_attn_Wq': _L0_attn_in['Wq'], 'L0_attn_bq': _L0_attn_in['bq'], 'L0_attn_Wk': _L0_attn_in['Wk'], 'L0_attn_bk': _L0_attn_in['bk'], 'L0_attn_Wv': _L0_attn_in['Wv'], 'L0_attn_bv': _L0_attn_in['bv'], 'L0_attn_Wo': _L0_attn_in['Wo'], 'L0_attn_bo': _L0_attn_in['bo'], 'L0_ffn_router_w': _L0_ffn_in['router_w'], 'L0_ffn_router_b': _L0_ffn_in['router_b'], 'L0_ffn_w1': _L0_ffn_in['w1'], 'L0_ffn_b1': _L0_ffn_in['b1'], 'L0_ffn_w2': _L0_ffn_in['w2'], 'L0_ffn_b2': _L0_ffn_in['b2']}

def reference(x, L0_tok_W, L0_tok_b, L0_tok_class_token, L0_tok_pos_embedding, L0_attn_Wq, L0_attn_bq, L0_attn_Wk, L0_attn_bk, L0_attn_Wv, L0_attn_bv, L0_attn_Wo, L0_attn_bo, L0_ffn_router_w, L0_ffn_router_b, L0_ffn_w1, L0_ffn_b1, L0_ffn_w2, L0_ffn_b2):
    import jax
    import jax.numpy as jnp

    def _L0_tok_ref(x, W, b, class_token, pos_embedding):
        import jax, jax.numpy as jnp
        import numpy as np
        P = 16

        def _patchify(x):
            B, C, H, W = x.shape
            gh, gw = (H // P, W // P)
            x = x.reshape(B, C, gh, P, gw, P)
            x = x.transpose(0, 2, 4, 1, 3, 5)
            return x.reshape(B, gh * gw, C * P * P)
        patches = _patchify(x)
        proj = jnp.einsum('bnk,dk->bnd', patches, W) + b
        B = x.shape[0]
        cls = jnp.broadcast_to(class_token, (B, 1, proj.shape[-1]))
        out = jnp.concatenate([cls, proj], axis=1) + pos_embedding
        return out

    def _L0_attn_ref(x, Wq, bq, Wk, bk, Wv, bv, Wo, bo):
        import jax, jax.numpy as jnp
        import numpy as np
        N_HEAD = 16
        Q_DIM = 64
        V_DIM = 64
        WINDOW = 129
        DIL = 1
        B, N, E = x.shape
        Q = (x @ Wq + bq).reshape(B, N, N_HEAD, Q_DIM).transpose(0, 2, 1, 3)
        K = (x @ Wk + bk).reshape(B, N, N_HEAD, Q_DIM).transpose(0, 2, 1, 3)
        V = (x @ Wv + bv).reshape(B, N, N_HEAD, V_DIM).transpose(0, 2, 1, 3)
        scores = jnp.einsum('bhid,bhjd->bhij', Q, K)
        idx = jnp.arange(N)
        diff = idx[None, :] - idx[:, None]
        half = WINDOW // 2
        band = (jnp.abs(diff) <= half * DIL) & (diff % DIL == 0)
        columns = jnp.where(band[None, None], scores, jnp.float32(0.0))
        attn = jax.nn.softmax(columns, axis=-1)
        out = attn @ V
        out = out.transpose(0, 2, 1, 3).reshape(B, N, N_HEAD * V_DIM)
        return out @ Wo + bo

    def _L0_ffn_ref(x, router_w, router_b, w1, b1, w2, b2):
        import math
        import jax, jax.numpy as jnp
        import numpy as np
        D_MODEL = 256
        D_HIDDEN = 1024
        N_EXPERTS = 8
        TOP_K = 2
        CAPACITY_FACTOR = 1.25
        B, T, D = x.shape
        N = B * T
        E = N_EXPERTS
        capacity = max(1, math.ceil(N / E * CAPACITY_FACTOR))
        x_flat = x.reshape(N, D)
        logits = x_flat.astype(jnp.float32) @ router_w + router_b
        gates = jax.nn.softmax(logits, axis=-1)
        _, topk_idx = jax.lax.top_k(gates, TOP_K)
        expert_mask = jax.nn.one_hot(topk_idx, E, dtype=jnp.int32).sum(1)
        pos = jnp.cumsum(expert_mask, axis=0) - 1
        expert_mask = expert_mask * (pos < capacity)
        valid = expert_mask > 0
        pos_c = jnp.where(valid, pos, capacity)
        e_idx = jnp.broadcast_to(jnp.arange(E), (N, E))
        dispatched = x_flat[:, None, :] * valid[:, :, None].astype(x.dtype)
        buf = jnp.zeros((E, capacity + 1, D), x.dtype).at[e_idx.ravel(), pos_c.ravel()].add(dispatched.reshape(N * E, D))
        buf = buf[:, :capacity]
        h = jax.nn.gelu(jnp.einsum('ecd,edh->ech', buf, w1) + b1[:, None, :], approximate=False)
        out = jnp.einsum('ech,ehd->ecd', h, w2) + b2[:, None, :]
        pos_g = jnp.minimum(pos_c, capacity - 1)
        gathered = out[e_idx, pos_g]
        weights = (gates * valid).astype(x.dtype)
        y = jnp.einsum('ned,ne->nd', gathered, weights)
        return y.reshape(B, T, D)
    h = _L0_tok_ref(x, L0_tok_W, L0_tok_b, L0_tok_class_token, L0_tok_pos_embedding)
    h = h + _L0_attn_ref(_layernorm(h, axis=-1), L0_attn_Wq, L0_attn_bq, L0_attn_Wk, L0_attn_bk, L0_attn_Wv, L0_attn_bv, L0_attn_Wo, L0_attn_bo)
    h = h + _L0_ffn_ref(_layernorm(h, axis=-1), L0_ffn_router_w, L0_ffn_router_b, L0_ffn_w1, L0_ffn_b1, L0_ffn_w2, L0_ffn_b2)
    return h

_drawn_inputs = setup_inputs


def setup_inputs(seed=0):
    import zlib

    import numpy as np

    out = dict(_drawn_inputs(seed))
    spreads = {'L0_ffn_router_b': (0.0, 0.285), 'L0_ffn_b1': (0.0, 0.584), 'L0_ffn_b2': (0.0, 0.1)}
    factors = {'L0_tok_class_token': 3.407, 'L0_attn_bq': 8.0, 'L0_attn_bk': 8.0}
    for name, (base, spread) in spreads.items():
        noise = np.random.default_rng([zlib.crc32(name.encode()), seed]).standard_normal(out[name].shape)
        drawn = base * np.exp(spread * noise) if base else spread * noise
        out[name] = jnp.asarray(drawn.astype(out[name].dtype))
    for name, factor in factors.items():
        out[name] = (out[name] * factor).astype(out[name].dtype)
    return out
```

```python
from contextlib import ExitStack

import concourse.bass as bass
from concourse import mybir

IMAGES, CHANNELS, SIDE, PATCH = 16, 3, 96, 16
GRID = SIDE // PATCH
SEQ = GRID * GRID + 1
TOKENS = IMAGES * SEQ
D = 256
DC = D // 128
PATCH_IN = CHANNELS * PATCH * PATCH
PC = PATCH_IN // 128
HEADS, HD = 16, 64
PAIRS = HEADS * HD // 128
EXPERTS, HIDDEN = 8, 1024
HC = HIDDEN // 128
CAP = -(-TOKENS * 5 // (EXPERTS * 4))
SLOTS = EXPERTS * CAP
HALF_SLOTS = SLOTS // 2
EMB_ROWS = SEQ + 2
TILES = [(s, min(128, TOKENS - s)) for s in range(0, TOKENS, 128)]
NT = len(TILES)
PER = 3
AT = [(s, min(PER * SEQ, TOKENS - s)) for s in range(0, TOKENS, PER * SEQ)]
W3 = PER * SEQ
HALF = TOKENS // 2
EPS = 1e-5
BIG = 2.0 ** 126

C_ID, C_TRI, C_ONE, C_SLOT, C_EXP, C_ML, C_MR, C_EPS, C_END = 0, 128, 256, 384, 480, 488, 600, 712, 720


def build(nc, patches, wT, emb, emb_sel, consts, wq, wk, wv, bqk, bv, wo, bo, rw, rb, w1, b1, w2, b2, out):
    f32, f32r, bf16, u32 = mybir.dt.float32, mybir.dt.float32r, mybir.dt.bfloat16, mybir.dt.uint32
    ALU, ACT, AX = mybir.AluOpType, mybir.ActivationFunctionType, mybir.AxisListType
    ctx = ExitStack()
    with ctx:
        def sem(name):
            return ctx.enter_context(nc.semaphore(name))

        arena = ctx.enter_context(nc.sbuf_tensor("arena", [128, 212736 // 4], f32))
        base = nc.sbuf_base - 212736
        at = [base]

        def region(n_bytes):
            start = at[0]
            at[0] += -(-n_bytes // 32) * 32
            assert at[0] <= base + 212736
            return start

        def sb(name, shape, dt, offset=None):
            n_bytes = 2 if dt == bf16 else 4
            for n in shape[1:]:
                n_bytes *= n
            return nc.alloc_sbuf_tensor_at(name, shape, dt, offset=region(n_bytes) if offset is None else offset)

        EXPERT_BYTES = 4 * (DC * HIDDEN + HC * D)
        r_own = [region(EXPERT_BYTES), region(EXPERT_BYTES)]
        r_qkvw = region(4 * 3 * DC * 1024)
        r_patch = region(4 * (NT * PC * 128 + PC * D))
        r_v = region(4 * len(AT) * 1024)
        r_qk = region(4 * 2 * PAIRS * TOKENS)
        r_e = region(4 * 4 * 8 * W3)
        r_lnT = region(4 * DC * TOKENS)
        r_ot = region(4 * PAIRS * TOKENS)

        w_raw = sb("w_raw", [128, 3, DC, 1024], f32, r_own[0])
        w_hi = sb("w_hi", [128, 3, DC, 1024], f32r, r_qkvw)
        wqk_lo = [sb(f"wqk_lo{o}", [128, 2, DC, 512], f32r, r_ot + o * 4 * PAIRS // 2 * TOKENS) for o in range(2)]
        wv_lo = sb("wv_lo", [128, DC, 1024], f32r, r_e)
        lnT_hi = sb("lnT_hi", [128, DC, TOKENS], f32r, r_lnT)
        lnT_lo = sb("lnT_lo", [128, DC, TOKENS], f32r, r_own[0] + 4 * 3 * DC * 1024)
        b2_sb = sb("b2_sb", [CAP, EXPERTS, D], f32, r_qkvw + EXPERT_BYTES)
        patches_sb = sb("patches_sb", [128, NT, PC, 128], f32, r_patch)
        wT_sb = sb("wT_sb", [128, PC, D], f32, r_patch + 4 * NT * PC * 128)
        v_sb = sb("v_sb", [W3, len(AT), 1024], f32, r_v)
        hidden_sb = sb("hidden_sb", [128, 2, HC, CAP], f32, r_v + EXPERT_BYTES)
        qT_sb = sb("qT_sb", [128, PAIRS, TOKENS], f32, r_qk)
        kT_sb = sb("kT_sb", [128, PAIRS, TOKENS], f32, r_qk + 4 * PAIRS * TOKENS)
        p_sb = sb("p_sb", [128, NT, EXPERTS, CAP], f32r, r_qk)
        pT_sb = sb("pT_sb", [CAP, EXPERTS, TOKENS], f32r, r_qk + 4 * PAIRS * TOKENS)
        e_sb = sb("e_sb", [W3, 2, 2, 4, W3], f32, r_e)
        eT_sb = sb("eT_sb", [W3, 2, 2, 4, W3], f32, r_e + 4 * 16 * W3)
        x_hi = sb("x_hi", [128, NT, D], f32r, r_e)
        x_lo = sb("x_lo", [128, NT, D], f32r, r_e + 4 * NT * D)
        oT_sb = sb("oT_sb", [128, PAIRS, TOKENS], f32, r_ot)
        xe_sb = sb("xe_sb", [128, DC, EXPERTS, CAP], f32, r_ot)
        y_at = r_ot + 4 * DC * SLOTS
        y_sb = sb("y_sb", [CAP, 2, D], f32, y_at)
        y_hi = sb("y_hi", [CAP, 2, D], f32r, y_at + 4 * 2 * D)
        y_lo = sb("y_lo", [CAP, 2, D], f32r, y_at + 4 * 4 * D)

        slot_at = [r_own[0], r_patch, r_v, r_own[1], r_qkvw, r_own[0], r_patch, r_v]
        w1_sb = [sb(f"w1_{e}", [128, DC, HIDDEN], f32, slot_at[e]) for e in range(EXPERTS)]
        w2_sb = [sb(f"w2_{e}", [128, HC, D], f32, slot_at[e] + 4 * DC * HIDDEN) for e in range(EXPERTS)]

        wo_sb = sb("wo_sb", [128, PAIRS, D], f32)
        ones_bf = sb("ones_bf", [128, 128], bf16)
        upto_bf = sb("upto_bf", [128, 128], bf16)
        bv_sb = sb("bv_sb", [W3, 1024], f32)
        bo_sb = sb("bo_sb", [128, D], f32)
        h_sb = sb("h_sb", [128, NT, D], f32)
        ln_sb = sb("ln_sb", [128, 3, D], f32)
        lnT_sb = sb("lnT_sb", [128, DC, TOKENS], f32, r_lnT)
        const_sb = sb("const_sb", [128, C_END], f32)
        maskL = sb("maskL", [128, W3], bf16)
        maskR = sb("maskR", [128, 4, W3], bf16)
        emb_sb = sb("emb_sb", [EMB_ROWS, D], f32)
        sel_sb = sb("sel_sb", [EMB_ROWS, TOKENS], f32)
        bqk_sb = sb("bqk_sb", [128, 2, PAIRS], f32)
        rw_sb = sb("rw_sb", [128, DC, EXPERTS], f32)
        rb_sb = sb("rb_sb", [1, EXPERTS], f32)
        b1_sb = sb("b1_sb", [128, EXPERTS, HC], f32)
        stats = sb("stats", [128, 2 * NT, 6], f32)
        mean_var = sb("mean_var", [128, 2 * NT, 2], f32)
        std = sb("std", [128, 2 * NT], f32)
        rstd = sb("rstd", [128, 2 * NT], f32)
        neg_max = sb("neg_max", [W3, 2, 2, 4], f32)
        row_sum = sb("row_sum", [W3, 2, 2, 4], f32)
        row_inv = sb("row_inv", [W3, 2, 2, 4], f32)
        logits = sb("logits", [128, NT, EXPERTS], f32)
        top8 = sb("top8", [128, NT, 8], f32)
        top_at = sb("top_at", [128, NT, 8], u32)
        first = sb("first", [128, NT, EXPERTS], f32)
        chosen = sb("chosen", [128, NT, EXPERTS], bf16)
        chosen_upto = sb("chosen_upto", [128, NT, EXPERTS], bf16)
        slot = sb("slot", [128, NT, EXPERTS], f32)
        shifted = sb("shifted", [128, NT, EXPERTS], f32)
        gate_exp = sb("gate_exp", [128, NT, EXPERTS], f32)
        gate_sum = sb("gate_sum", [128, NT], f32)
        gate_inv = sb("gate_inv", [128, NT], f32)
        gates = sb("gates", [128, NT, EXPERTS], f32)
        gate_parts = sb("gate_parts", [128, NT, 2, EXPERTS], f32r)
        gate_rows = sb("gate_rows", [2 * EXPERTS, EXPERTS, CAP], f32, r_e + 4 * 2 * NT * D)
        slot_gate_hi = sb("slot_gate_hi", [CAP, EXPERTS], f32)
        slot_gate = sb("slot_gate", [CAP, EXPERTS], f32)

        bank = [ctx.enter_context(nc.psum_tensor(f"bank{i}", [128, 512], f32)) for i in range(8)]

        ident = const_sb[:, C_ID:C_ID + 128]
        ones = const_sb[:, C_ONE:C_ONE + 128]
        slot_no = const_sb[:, C_SLOT:C_SLOT + CAP]
        expert_no = const_sb[:, C_EXP:C_EXP + EXPERTS]
        eps = const_sb[:, C_EPS:C_EPS + 1]

        def sems(names):
            return [sem(n) for n in names.split()]

        const_in, emb_in, bv_in, bqk_in, wo_in, bo_in, router_in, b1_in, b2_in = sems(
            "const_in emb_in bv_in bqk_in wo_in bo_in router_in b1_in b2_in")
        wT_in = [sem(f"wT_in{i}") for i in range(2)]
        patch0_in = [sem(f"patch0_in{i}") for i in range(2)]
        patches_in = [None] + [sem(f"patches_in{t}") for t in range(1, NT)]
        w_in = [sem(f"w_in{i}") for i in range(3)]
        expert_in = [sem(f"expert_in{e}") for e in range(EXPERTS)]
        out_sent = sem("out_sent")
        (patch_mm, ln_T, v_mm, qk_mm, scores_mm, e_T, pv_mm, wo_mm, router_mm, count_mm, dispatch_mm, gate_mm,
         gate_T, p_T, up_mm, down_mm, combine_mm, y_final) = sems(
            "patch_mm ln_T v_mm qk_mm scores_mm e_T pv_mm wo_mm router_mm count_mm dispatch_mm gate_mm "
            "gate_T p_T up_mm down_mm combine_mm y_final")
        (h_ready, std_ready, lnT_hi_ready, lnT_ready, qk0_ready, exp_ready, oT_ready, pT_ready, gate_exp_ready,
         xe0_ready, gate_rows_ready, gelu_ready) = sems(
            "h_ready std_ready lnT_hi_ready lnT_ready qk0_ready exp_ready oT_ready pT_ready gate_exp_ready "
            "xe0_ready gate_rows_ready gelu_ready")
        (bf_ready, stats_ready, mv_ready, rstd_ready, ln_ready, lnT_lo_ready, w_hi_ready, v_ready, qk1_ready,
         max_ready, inv_ready, eT_ready, h2_ready, top_ready, top_at_ready, first_ready, chosen_ready, logits_ready,
         slot_ready, p_ready, shifted_ready, gate_sum_ready, gate_inv_ready, gates_ready, gate_hi_ready,
         gate_lo_ready, xe1_ready, slot_gate_hi_ready, slot_gate_ready, y_biased, y_hi_ready, y_ready, out_ready) = sems(
            "bf_ready stats_ready mv_ready rstd_ready ln_ready lnT_lo_ready w_hi_ready v_ready qk1_ready "
            "max_ready inv_ready eT_ready h2_ready top_ready top_at_ready first_ready chosen_ready logits_ready "
            "slot_ready p_ready shifted_ready gate_sum_ready gate_inv_ready gates_ready gate_hi_ready "
            "gate_lo_ready xe1_ready slot_gate_hi_ready slot_gate_ready y_biased y_hi_ready y_ready out_ready")
        zero_ready, w_lo_ready, hb_ready, norm_ready, x_hi_ready, x_lo_ready, upto_ready = sems(
            "zero_ready w_lo_ready hb_ready norm_ready x_hi_ready x_lo_ready upto_ready")

        V_BANKS, QK_BANKS, LATE_QK_BANK = [0, 1, 2], [3, 4, 7], 7
        EMBED_BANKS = range(NT)
        E_BANKS, OUT_BANK = [4, 5], 6
        WO_BANKS = [7, 7, 0, 7, 3]
        ROUTER_BANKS = [1, 2, 0, 3, 4]
        LOGIT_COLS, COUNT_COLS = slice(0, EXPERTS), slice(EXPERTS, 2 * EXPERTS)
        XE_BANKS = [[0, 1], [2, 7]]
        P_BANK, GATE_BANKS, GATE_T_BANK = 6, [3, 4], 3
        UP_BANKS, DOWN_BANKS = [7, 4], [5, 6]

        def lnT_bank(i):
            return bank[5 + i % 2 if i < NT else 5]

        def score_bank(g, b):
            return bank[2 * (g % 2) + b]

        GROUPS = [(o, a) for o in range(2) for a in range(len(AT))]
        NG = len(GROUPS)
        QK_UNITS = [(pair, which, half) for pair in range(PAIRS) for which in range(2) for half in range(2)]
        EARLY = len(QK_UNITS) // 2
        LATE_AT = [list(range(EARLY + 3 * s, min(EARLY + 3 * s + 3, len(QK_UNITS)))) for s in range(len(AT))]
        WO_AT = {NG - 2 + t: t for t in range(NT - 1)}
        W_PIECES = [(i, c, half) for i in (2, 0, 1) for c in range(DC) for half in range(2)]
        V_PIECES = 4

        def late_unit(step, k):
            units = LATE_AT[step] if step < len(LATE_AT) else []
            return units[k] if k < len(units) else None

        block = ctx.enter_context(nc.Block())

        @block.sync
        def _(sp):
            for i in range(2):
                cs = slice(i * PC // 2, (i + 1) * PC // 2)
                sp.dma_start(patches_sb[:, 0, cs, :], patches[:, 0, cs, :]).then_inc(patch0_in[i], 16)
            for t in range(1, NT):
                sp.dma_start(patches_sb[:, t, :, :], patches[:, t, :, :]).then_inc(patches_in[t], 16)
            for i, w in ((2, wv), (0, wq), (1, wk)):
                sp.dma_start(w_raw[:, i, :, :], w.rearrange("(c p) n -> p c n", p=128)).then_inc(w_in[i], 16)
            sp.dma_start(wo_sb[:, :, :], wo.rearrange("(c p) n -> p c n", p=128)).then_inc(wo_in, 16)

            def load_expert(e):
                sp.dma_start(w1_sb[e][:, :, :], w1[e].rearrange("(c p) n -> p c n", p=128)).then_inc(expert_in[e], 16)
                sp.dma_start(w2_sb[e][:, :, :], w2[e].rearrange("(c p) n -> p c n", p=128)).then_inc(expert_in[e], 16)

            sp.wait_ge(patch_mm, NT)
            load_expert(1)
            sp.wait_ge(w_lo_ready, len(W_PIECES))
            load_expert(0)
            sp.wait_ge(v_mm, 2 * len(AT))
            sp.wait_ge(qk_mm, len(QK_UNITS))
            load_expert(3)
            load_expert(4)
            sp.dma_start(b2_sb[:, :, :], b2.unsqueeze(0).to_broadcast([CAP, EXPERTS, D])).then_inc(b2_in, 16)
            sp.wait_ge(pv_mm, NG)
            load_expert(2)
            for e, used in ((5, 0), (6, 1), (7, 2)):
                sp.wait_ge(down_mm, used + 1)
                load_expert(e)
            for t, (s, n) in enumerate(TILES):
                sp.wait_ge(out_ready, t + 1)
                sp.dma_start(out[s:s + n, :], h_sb[0:n, t, :]).then_inc(out_sent, 16)
            sp.wait_ge(out_sent, 16 * NT)

        @block.gpsimd
        def _(pool):
            pool.dma_start(bv_sb[:, :], bv.unsqueeze(0).to_broadcast([W3, 1024])).then_inc(bv_in, 16)
            pool.dma_start(bqk_sb[:, :, :], bqk).then_inc(bqk_in, 16)
            pool.dma_start(bo_sb[:, :], bo.unsqueeze(0).to_broadcast([128, D])).then_inc(bo_in, 16)
            pool.dma_start(rw_sb[:, :, :], rw.rearrange("(c p) n -> p c n", p=128)).then_inc(router_in, 16)
            pool.dma_start(rb_sb[:, :], rb.unsqueeze(0)).then_inc(router_in, 16)
            pool.dma_start(b1_sb[:, :, :], b1).then_inc(b1_in, 16)
            pool.memset(logits[:, :, :], 0.0).then_inc(zero_ready, 1)
            pool.memset(top8[:, :, :], 0.0).then_inc(zero_ready, 1)
            for k, (i, c, half) in enumerate(W_PIECES):
                cols = slice(half * 512, (half + 1) * 512)
                pool.wait_ge(w_hi_ready, k + 1)
                lo = wv_lo[:, c, cols] if i == 2 else wqk_lo[half][:, i, c, :]
                pool.tensor_tensor(lo, w_raw[:, i, c, cols], w_hi[:, i, c, cols].bitcast(f32), ALU.subtract)\
                    .then_inc(w_lo_ready, 1)
            pool.wait_ge(bo_in, 16)
            for t, (s, n) in enumerate(TILES):
                pool.wait_ge(ln_ready, t + 1)
                pool.tensor_tensor(h_sb[0:n, t, :], h_sb[0:n, t, :], bo_sb[0:n, :], ALU.add).then_inc(hb_ready, 1)
            for g, (o, a) in enumerate(GROUPS):
                n = AT[a][1]
                for b in range(2):
                    pool.wait_ge(inv_ready, 2 * g + b + 1)
                    e = e_sb[0:n, g % 2, b, :, 0:n]
                    pool.tensor_tensor(e, e, row_inv[0:n, g % 2, b, :].unsqueeze(2).to_broadcast([n, 4, n]),
                                       ALU.mult).then_inc(norm_ready, 1)

            def split_x(t):
                n = TILES[t][1]
                x = ln_sb[0:n, (NT + t) % 3, :]
                pool.wait_ge(ln_ready, NT + t + 1)
                pool.tensor_copy(x_hi[0:n, t, :], x).then_inc(x_hi_ready, 1)
                pool.wait_ge(x_hi_ready, t + 1)
                pool.tensor_tensor(x_lo[0:n, t, :], x, x_hi[0:n, t, :].bitcast(f32), ALU.subtract).then_inc(x_lo_ready, 1)

            def sum_chosen(t):
                n = TILES[t][1]
                pool.wait_ge(chosen_ready, t + 1)
                if t == 0:
                    pool.tensor_copy(chosen_upto[:, 0, :], chosen[:, 0, :]).then_inc(upto_ready, 1)
                else:
                    pool.wait_ge(upto_ready, t)
                    pool.tensor_tensor(chosen_upto[:, t, :], chosen_upto[:, t - 1, :], chosen[:, t, :],
                                       ALU.add).then_inc(upto_ready, 1)

            pool.wait_ge(e_T, 2 * NG)
            pool.wait_ge(pv_mm, NG)
            split_x(0)
            split_x(1)
            split_x(2)
            sum_chosen(0)
            split_x(3)
            sum_chosen(1)
            split_x(4)
            sum_chosen(2)
            sum_chosen(3)

        @block.scalar
        def _(act):
            for i in range(2):
                cs = slice(i * PC // 2, (i + 1) * PC // 2)
                act.dma_start(wT_sb[:, cs, :], wT[:, cs, :]).then_inc(wT_in[i], 16)
            act.dma_start(emb_sb[:, :], emb).then_inc(emb_in, 16)
            act.dma_start(sel_sb[:, :], emb_sel).then_inc(emb_in, 16)
            act.dma_start(const_sb[:, :], consts).then_inc(const_in, 16)

            def std_of(i):
                n = TILES[i % NT][1]
                act.wait_ge(mv_ready, i + 1)
                act.activation(std[0:n, i:i + 1], mean_var[0:n, i, 1:2], ACT.Sqrt, bias=eps[0:n, :]).then_inc(std_ready, 1)

            def copy_lnT(i):
                s, n = TILES[i % NT]
                act.wait_ge(ln_T, i + 1)
                src = lnT_bank(i)[:, 0:D].rearrange("p (c n) -> p c n", c=DC)[:, :, 0:n]
                if i < NT:
                    act.activation(lnT_hi[:, :, s:s + n], src, ACT.Copy).then_inc(lnT_hi_ready, 1)
                else:
                    act.activation(lnT_sb[:, :, s:s + n], src, ACT.Copy).then_inc(lnT_ready, 1)

            act.wait_ge(const_in, 16)
            for t, (s, n) in enumerate(TILES):
                act.wait_ge(patch_mm, t + 1)
                act.activation(h_sb[0:n, t, :], bank[EMBED_BANKS[t]][0:n, 0:D], ACT.Copy).then_inc(h_ready, 1)
                std_of(t)
                if t >= 1:
                    copy_lnT(t - 1)
            copy_lnT(NT - 1)
            act.wait_ge(bqk_in, 16)
            for u in range(EARLY):
                pair, which, half = QK_UNITS[u]
                act.wait_ge(qk_mm, u + 1)
                act.activation((qT_sb, kT_sb)[which][:, pair, half * HALF:(half + 1) * HALF],
                               bank[QK_BANKS[u % 3]][:, 0:HALF], ACT.Identity,
                               bias=bqk_sb[:, which, pair:pair + 1]).then_inc(qk0_ready, 1)

            def exps(g):
                n = AT[GROUPS[g][1]][1]
                if g >= 2:
                    act.wait_ge(e_T, 2 * (g - 1))
                for b in range(2):
                    act.wait_ge(max_ready, 2 * g + b + 1)
                    for j in range(4):
                        act.activation(e_sb[0:n, g % 2, b, j, 0:n], score_bank(g, b)[0:n, j * W3:j * W3 + n], ACT.Exp,
                                       bias=neg_max[0:n, g % 2, b, j:j + 1],
                                       accum_out=row_sum[0:n, g % 2, b, j:j + 1]).then_inc(exp_ready, 1)

            def copy_oT(g):
                o, a = GROUPS[g]
                s, n = AT[a]
                act.wait_ge(pv_mm, g + 1)
                act.activation(oT_sb[:, 4 * o:4 * o + 4, s:s + n],
                               bank[OUT_BANK][:, 0:4 * W3].rearrange("p (j n) -> p j n", j=4)[:, :, 0:n],
                               ACT.Copy).then_inc(oT_ready, 1)

            for step in range(NG):
                exps(step)
                if step >= 2:
                    copy_oT(step - 2)
            copy_oT(NG - 2)
            std_of(NT)
            std_of(NT + 1)
            std_of(NT + 2)
            copy_lnT(NT)
            copy_oT(NG - 1)
            std_of(NT + 3)
            copy_lnT(NT + 1)
            copy_lnT(NT + 2)
            std_of(NT + 4)
            copy_lnT(NT + 3)

            def copy_pT(t, q):
                s, n = TILES[t]
                act.wait_ge(p_T, 2 * t + q + 1)
                act.activation(pT_sb[:, 4 * q:4 * q + 4, s:s + n],
                               bank[P_BANK][0:CAP, :].rearrange("p (e n) -> p e n", e=4)[:, :, 0:n],
                               ACT.Copy).then_inc(pT_ready, 1)

            copy_pT(0, 0)
            copy_lnT(NT + 4)
            for t, q in ((0, 1), (1, 0), (1, 1), (2, 0), (2, 1), (3, 0)):
                copy_pT(t, q)
            act.wait_ge(shifted_ready, 1)
            act.activation(gate_exp[:, :, :], shifted[:, :, :], ACT.Exp).then_inc(gate_exp_ready, 1)
            copy_pT(3, 1)
            act.wait_ge(dispatch_mm, NT)
            for half in range(2):
                act.activation(xe_sb[:, 0, 4 * half:4 * half + 4, :],
                               bank[XE_BANKS[0][half]][:, 0:HALF_SLOTS].rearrange("p (e c) -> p e c", e=4),
                               ACT.Copy).then_inc(xe0_ready, 1)
            copy_pT(4, 0)
            act.wait_ge(gate_mm, 1)
            for half in range(2):
                act.activation(gate_rows[:, 4 * half:4 * half + 4, :],
                               bank[GATE_BANKS[half]][0:2 * EXPERTS, 0:HALF_SLOTS].rearrange("p (e c) -> p e c", e=4),
                               ACT.Copy).then_inc(gate_rows_ready, 1)
            copy_pT(4, 1)

            act.wait_ge(b1_in, 16)
            for e in range(EXPERTS):
                if e >= 2:
                    act.wait_ge(down_mm, e - 1)
                for q in range(2):
                    act.wait_ge(up_mm, 2 * e + q + 1)
                    for k in range(4):
                        c = 4 * q + k
                        act.activation(hidden_sb[:, e % 2, c, :], bank[UP_BANKS[q]][:, k * CAP:(k + 1) * CAP],
                                       ACT.Gelu, bias=b1_sb[:, e, c:c + 1]).then_inc(gelu_ready, 1)

        @block.vector
        def _(dve):
            def moments(i):
                t = i % NT
                n = TILES[t][1]
                dve.bn_stats(stats[0:n, i, :], h_sb[0:n, t, :]).then_inc(stats_ready, 1)
                dve.wait_ge(stats_ready, i + 1)
                dve.bn_aggr(mean_var[0:n, i, :], stats[0:n, i, :]).then_inc(mv_ready, 1)

            def normalise(i):
                t = i % NT
                n = TILES[t][1]
                dve.wait_ge(std_ready, i + 1)
                dve.reciprocal(rstd[0:n, i:i + 1], std[0:n, i:i + 1]).then_inc(rstd_ready, 1)
                dve.wait_ge(rstd_ready, i + 1)
                if i >= 3:
                    dve.wait_ge(ln_T, i - 2)
                if i >= NT + 3:
                    dve.wait_ge(x_lo_ready, i - NT - 2)
                dve.tensor_scalar(ln_sb[0:n, i % 3, :], h_sb[0:n, t, :], mean_var[0:n, i, 0:1],
                                  rstd[0:n, i:i + 1], ALU.subtract, ALU.mult).then_inc(ln_ready, 1)

            def lnT_low(t):
                s, n = TILES[t]
                dve.wait_ge(lnT_hi_ready, t + 1)
                dve.tensor_tensor(lnT_lo[:, :, s:s + n],
                                  lnT_bank(t)[:, 0:D].rearrange("p (c n) -> p c n", c=DC)[:, :, 0:n],
                                  lnT_hi[:, :, s:s + n].bitcast(f32), ALU.subtract).then_inc(lnT_lo_ready, 1)

            def weight_high(k):
                i, c, half = W_PIECES[k]
                cols = slice(half * 512, (half + 1) * 512)
                dve.wait_ge(w_in[i], 16)
                dve.tensor_copy(w_hi[:, i, c, cols], w_raw[:, i, c, cols]).then_inc(w_hi_ready, 1)

            for t in range(NT):
                dve.wait_ge(h_ready, t + 1)
                moments(t)
                if t >= 1:
                    lnT_low(t - 1)
                normalise(t)
                if t == 2:
                    dve.wait_ge(const_in, 16)
                    for j in range(4):
                        dve.tensor_copy(maskR[:, j, :], const_sb[:, C_MR:C_MR + W3]).then_inc(bf_ready, 1)
                    dve.tensor_copy(maskL[:, :], const_sb[:, C_ML:C_ML + W3]).then_inc(bf_ready, 1)
                    dve.tensor_copy(ones_bf[:, :], ones).then_inc(bf_ready, 1)
                    dve.tensor_copy(upto_bf[:, :], const_sb[:, C_TRI:C_TRI + 128]).then_inc(bf_ready, 1)
                if t == 3:
                    for k in range(V_PIECES):
                        weight_high(k)
            lnT_low(NT - 1)
            dve.wait_ge(bv_in, 16)
            for u in range(2 * len(AT)):
                a, half = u // 2, u % 2
                n = AT[a][1]
                if V_PIECES + u < len(W_PIECES):
                    weight_high(V_PIECES + u)
                dve.wait_ge(v_mm, u + 1)
                dve.tensor_tensor(v_sb[0:n, a, half * 512:(half + 1) * 512], bank[V_BANKS[u % 3]][0:n, :],
                                  bv_sb[0:n, half * 512:(half + 1) * 512], ALU.add).then_inc(v_ready, 1)

            def row_max(g):
                n = AT[GROUPS[g][1]][1]
                for b in range(2):
                    dve.wait_ge(scores_mm, 2 * g + b + 1)
                    if g >= 2:
                        dve.wait_ge(exp_ready, 8 * (g - 2) + 4 * (b + 1))
                    dve.tensor_reduce(neg_max[0:n, g % 2, b, :],
                                      score_bank(g, b)[0:n, 0:4 * W3].rearrange("p (j n) -> p j n", j=4)[:, :, 0:n],
                                      AX.X, ALU.max, negate=True).then_inc(max_ready, 1)

            def copy_eT(g):
                n = AT[GROUPS[g][1]][1]
                if g >= 2:
                    dve.wait_ge(pv_mm, g - 1)
                for b in range(2):
                    dve.wait_ge(e_T, 2 * g + b + 1)
                    dve.tensor_copy(eT_sb[0:n, g % 2, b, :, 0:n],
                                    bank[E_BANKS[b]][0:n, 0:4 * W3].rearrange("p (j n) -> p j n", j=4)[:, :, 0:n])\
                       .then_inc(eT_ready, 1)

            def inverse_sums(g):
                n = AT[GROUPS[g][1]][1]
                for b in range(2):
                    dve.wait_ge(exp_ready, 8 * g + 4 * (b + 1))
                    if g >= 2:
                        dve.wait_ge(norm_ready, 2 * (g - 2) + b + 1)
                    dve.reciprocal(row_inv[0:n, g % 2, b, :], row_sum[0:n, g % 2, b, :]).then_inc(inv_ready, 1)

            def late_qk(u):
                if u is not None:
                    pair, which, half = QK_UNITS[u]
                    dve.wait_ge(qk_mm, u + 1)
                    dve.tensor_scalar((qT_sb, kT_sb)[which][:, pair, half * HALF:(half + 1) * HALF],
                                      bank[LATE_QK_BANK][:, 0:HALF], bqk_sb[:, which, pair:pair + 1], None,
                                      ALU.add).then_inc(qk1_ready, 1)

            def residual(t):
                s, n = TILES[t]
                dve.wait_ge(wo_mm, t + 1)
                dve.wait_ge(hb_ready, t + 1)
                dve.tensor_tensor(h_sb[0:n, t, :], h_sb[0:n, t, :], bank[WO_BANKS[t]][0:n, 0:D], ALU.add)\
                   .then_inc(h2_ready, 1)
                dve.wait_ge(h2_ready, t + 1)
                moments(NT + t)

            dve.wait_ge(bqk_in, 16)
            for step in range(NG + 2):
                if step < NG:
                    row_max(step)
                late_qk(late_unit(step, 0))
                if step in WO_AT:
                    residual(WO_AT[step])
                if 1 <= step <= NG:
                    copy_eT(step - 1)
                late_qk(late_unit(step, 1))
                if step < NG:
                    inverse_sums(step)
                late_qk(late_unit(step, 2))
                if step == NG:
                    normalise(NT)
                    normalise(NT + 1)

            def choose(t):
                n = TILES[t][1]
                now = bank[ROUTER_BANKS[t]][0:n, LOGIT_COLS]
                dve.wait_ge(router_mm, t + 1)
                dve.max(top8[0:n, t, :], now).then_inc(top_ready, 1)
                dve.wait_ge(top_ready, t + 1)
                dve.max_index(top_at[0:n, t, :], top8[0:n, t, :], now).then_inc(top_at_ready, 1)
                dve.wait_ge(top_at_ready, t + 1)
                dve.tensor_scalar(first[0:n, t, :], expert_no[0:n, :], top_at[0:n, t, 0:1], None,
                                  ALU.is_equal).then_inc(first_ready, 1)
                dve.wait_ge(first_ready, t + 1)
                dve.scalar_tensor_tensor(chosen[0:n, t, :], expert_no[0:n, :], top_at[0:n, t, 1:2],
                                         first[0:n, t, :], ALU.is_equal, ALU.add).then_inc(chosen_ready, 1)
                dve.tensor_copy(logits[0:n, t, :], now).then_inc(logits_ready, 1)

            def place(t):
                n = TILES[t][1]
                dve.wait_ge(count_mm, t + 1)
                dve.wait_ge(chosen_ready, t + 1)
                dve.tensor_tensor(slot[0:n, t, :], bank[ROUTER_BANKS[t]][0:n, COUNT_COLS], chosen[0:n, t, :],
                                  ALU.mult).then_inc(slot_ready, 1)
                dve.wait_ge(slot_ready, t + 1)
                dve.tensor_tensor(p_sb[0:n, t, :, :], slot_no[0:n, :].unsqueeze(1).to_broadcast([n, EXPERTS, CAP]),
                                  slot[0:n, t, :].unsqueeze(2).to_broadcast([n, EXPERTS, CAP]),
                                  ALU.is_equal).then_inc(p_ready, 1)

            normalise(NT + 2)
            dve.wait_ge(zero_ready, 2)
            choose(0)
            normalise(NT + 3)
            residual(4)
            choose(1)
            place(0)
            normalise(NT + 4)
            choose(2)
            place(1)
            choose(3)
            place(2)
            choose(4)
            dve.wait_ge(logits_ready, NT)
            dve.tensor_tensor(shifted[:, :, :], logits[:, :, :], top8[:, :, 0:1].to_broadcast([128, NT, EXPERTS]),
                              ALU.subtract).then_inc(shifted_ready, 1)
            place(3)
            place(4)
            dve.wait_ge(gate_exp_ready, 1)
            dve.tensor_reduce(gate_sum[:, :], gate_exp[:, :, :], AX.X, ALU.add).then_inc(gate_sum_ready, 1)
            dve.wait_ge(gate_sum_ready, 1)
            dve.reciprocal(gate_inv[:, :], gate_sum[:, :]).then_inc(gate_inv_ready, 1)
            dve.wait_ge(gate_inv_ready, 1)
            dve.tensor_tensor(gates[:, :, :], gate_exp[:, :, :],
                              gate_inv[:, :].unsqueeze(2).to_broadcast([128, NT, EXPERTS]), ALU.mult).then_inc(gates_ready, 1)
            dve.wait_ge(gates_ready, 1)
            dve.tensor_copy(gate_parts[:, :, 0, :], gates[:, :, :]).then_inc(gate_hi_ready, 1)
            dve.wait_ge(gate_hi_ready, 1)
            dve.tensor_tensor(gate_parts[:, :, 1, :], gates[:, :, :], gate_parts[:, :, 0, :].bitcast(f32),
                              ALU.subtract).then_inc(gate_lo_ready, 1)

            dve.wait_ge(dispatch_mm, NT)
            for half in range(2):
                dve.tensor_copy(xe_sb[:, 1, 4 * half:4 * half + 4, :],
                                bank[XE_BANKS[1][half]][:, 0:HALF_SLOTS].rearrange("p (e c) -> p e c", e=4))\
                   .then_inc(xe1_ready, 1)
            dve.wait_ge(gate_T, 1)
            picked = bank[GATE_T_BANK][0:CAP, 0:EXPERTS * 2 * EXPERTS]
            step_e = 2 * EXPERTS + 1
            dve.tensor_copy(slot_gate_hi[:, :], picked[:, 0::step_e]).then_inc(slot_gate_hi_ready, 1)
            dve.wait_ge(slot_gate_hi_ready, 1)
            dve.tensor_tensor(slot_gate[:, :], slot_gate_hi[:, :], picked[:, EXPERTS::step_e], ALU.add)\
               .then_inc(slot_gate_ready, 1)

            dve.wait_ge(slot_gate_ready, 1)
            dve.wait_ge(b2_in, 16)
            for e in range(EXPERTS):
                dve.wait_ge(down_mm, e + 1)
                if e >= 2:
                    dve.wait_ge(y_ready, e - 1)
                dve.tensor_tensor(y_sb[:, e % 2, :], bank[DOWN_BANKS[e % 2]][0:CAP, 0:D], b2_sb[:, e, :],
                                  ALU.add).then_inc(y_biased, 1)
                dve.wait_ge(y_biased, e + 1)
                if e >= 2:
                    dve.wait_ge(combine_mm, e - 1)
                dve.tensor_scalar(y_hi[:, e % 2, :], y_sb[:, e % 2, :], slot_gate[:, e:e + 1], None,
                                  ALU.mult).then_inc(y_hi_ready, 1)
                dve.wait_ge(y_hi_ready, e + 1)
                dve.scalar_tensor_tensor(y_lo[:, e % 2, :], y_sb[:, e % 2, :], slot_gate[:, e:e + 1],
                                         y_hi[:, e % 2, :].bitcast(f32), ALU.mult, ALU.subtract).then_inc(y_ready, 1)
            for t, (s, n) in enumerate(TILES):
                dve.wait_ge(y_final, t // 2 + 1)
                dve.tensor_tensor(h_sb[0:n, t, :], h_sb[0:n, t, :], bank[t // 2][0:n, (t % 2) * D:(t % 2 + 1) * D],
                                  ALU.add).then_inc(out_ready, 1)

        @block.tensor
        def _(pe):
            mm = pe.matmul

            def embed(t):
                s, n = TILES[t]
                dst = bank[EMBED_BANKS[t]][0:n, 0:D]
                if t:
                    pe.wait_ge(patches_in[t], 16)
                for c in range(PC):
                    if t == 0 and c % (PC // 2) == 0:
                        pe.wait_ge(patch0_in[c // (PC // 2)], 16)
                        pe.wait_ge(wT_in[c // (PC // 2)], 16)
                    mm(dst, patches_sb[:, t, c, 0:n], wT_sb[:, c, :], start=c == 0, stop=False)
                if t == 0:
                    pe.wait_ge(emb_in, 32)
                mm(dst, sel_sb[:, s:s + n], emb_sb[:, :], start=False, stop=True).then_inc(patch_mm, 1)

            def transpose_ln(i):
                t = i % NT
                n = TILES[t][1]
                pe.wait_ge(ln_ready, i + 1)
                if 2 <= i < NT:
                    pe.wait_ge(lnT_lo_ready, i - 1)
                if i > NT:
                    pe.wait_ge(lnT_ready, i - NT)
                for c in range(DC):
                    last = pe.transpose(lnT_bank(i)[:, c * 128:c * 128 + n], ln_sb[0:n, i % 3, c * 128:(c + 1) * 128],
                                        ident[0:n, 0:n])
                last.then_inc(ln_T, 1)

            def project_v(a):
                s, n = AT[a]
                pe.wait_ge(lnT_lo_ready, (s + n - 1) // 128 + 1)
                for half in range(2):
                    u = 2 * a + half
                    cols = slice(half * 512, (half + 1) * 512)
                    if u >= 3:
                        pe.wait_ge(v_ready, u - 2)
                    for c in range(DC):
                        parts = ((lnT_hi, w_hi[:, 2, c, cols]), (lnT_hi, wv_lo[:, c, cols]), (lnT_lo, w_hi[:, 2, c, cols]))
                        for k, (x, w) in enumerate(parts):
                            last = mm(bank[V_BANKS[u % 3]][0:n, :], x[:, c, s:s + n], w,
                                      start=c == 0 and k == 0, stop=c == DC - 1 and k == 2)
                    last.then_inc(v_mm, 1)

            def project_qk(u):
                if u is None:
                    return
                pair, which, half = QK_UNITS[u]
                if u < EARLY:
                    dst = bank[QK_BANKS[u % 3]][:, 0:HALF]
                    if u >= 3:
                        pe.wait_ge(qk0_ready, u - 2)
                else:
                    dst = bank[LATE_QK_BANK][:, 0:HALF]
                    if u == EARLY:
                        pe.wait_ge(qk0_ready, EARLY)
                    else:
                        pe.wait_ge(qk1_ready, u - EARLY)
                tokens, rows = slice(half * HALF, (half + 1) * HALF), slice(pair * 128, (pair + 1) * 128)
                lo_rows = slice(pair % 4 * 128, (pair % 4 + 1) * 128)
                for c in range(DC):
                    hi, lo = w_hi[:, which, c, rows], wqk_lo[pair // 4][:, which, c, lo_rows]
                    for k, (w, x) in enumerate(((hi, lnT_hi), (hi, lnT_lo), (lo, lnT_hi))):
                        last = mm(dst, w, x[:, c, tokens], start=c == 0 and k == 0, stop=c == DC - 1 and k == 2)
                last.then_inc(qk_mm, 1)

            embed(0)
            pe.wait_ge(const_in, 16)
            for t in range(1, NT):
                embed(t)
                transpose_ln(t - 1)
            pe.wait_ge(w_lo_ready, V_PIECES)
            pe.wait_ge(h_ready, NT)
            project_v(0)
            transpose_ln(NT - 1)
            for a in range(1, len(AT)):
                project_v(a)
            pe.wait_ge(w_lo_ready, len(W_PIECES))
            for u in range(EARLY):
                project_qk(u)

            def scores(g):
                o, a = GROUPS[g]
                s, n = AT[a]
                masked = n > SEQ
                both = [slice(0, 64), slice(64, 128)]
                for b, rows in enumerate(both):
                    if g >= 2:
                        pe.wait_ge(exp_ready, 8 * (g - 2) + 4 * (b + 1))
                    if masked:
                        mm(score_bank(g, b)[0:n, 0:4 * W3], maskL[rows, :], maskR[rows, :, :].rearrange("p j n -> p (j n)"),
                           start=True, stop=False)
                for j in range(4):
                    for b, rows in enumerate(both):
                        last = mm(score_bank(g, b)[0:n, j * W3:j * W3 + n], qT_sb[rows, 4 * o + j, s:s + n],
                                  kT_sb[rows, 4 * o + j, s:s + n], start=not masked, stop=j == 3 or not masked)
                        if j == 3:
                            last.then_inc(scores_mm, 1)

            def transpose_e(g):
                n = AT[GROUPS[g][1]][1]
                for b in range(2):
                    pe.wait_ge(norm_ready, 2 * g + b + 1)
                    if g >= 1:
                        pe.wait_ge(eT_ready, 2 * (g - 1) + b + 1)
                    for j in range(4):
                        last = pe.transpose(bank[E_BANKS[b]][0:n, j * W3:j * W3 + n], e_sb[0:n, g % 2, b, j, 0:n],
                                            ident[0:n, 0:n])
                    last.then_inc(e_T, 1)

            def weigh_v(g):
                o, a = GROUPS[g]
                n = AT[a][1]
                pe.wait_ge(eT_ready, 2 * g + 2)
                if g >= 1:
                    pe.wait_ge(oT_ready, g)
                for j in range(4):
                    for b in range(2):
                        head = 2 * (4 * o + j) + b
                        last = mm(bank[OUT_BANK][64 * b:64 * b + 64, j * W3:j * W3 + n],
                                  v_sb[0:n, a, head * HD:(head + 1) * HD], eT_sb[0:n, g % 2, b, j, 0:n],
                                  start=True, stop=True)
                last.then_inc(pv_mm, 1)

            def project_out(t):
                s, n = TILES[t]
                pe.wait_ge(oT_ready, len(AT) + (s + n - 1) // W3 + 1)
                if WO_BANKS[t] == 7:
                    if t == 0:
                        pe.wait_ge(qk1_ready, len(QK_UNITS) - EARLY)
                    else:
                        pe.wait_ge(h2_ready, t if t == 1 else t - 1)
                else:
                    pe.wait_ge(exp_ready, 8 * (NG - 1) if WO_BANKS[t] < 2 else 8 * NG)
                for c in range(PAIRS):
                    last = mm(bank[WO_BANKS[t]][0:n, 0:D], oT_sb[:, c, s:s + n], wo_sb[:, c, :],
                              start=c == 0, stop=c == PAIRS - 1)
                last.then_inc(wo_mm, 1)

            def route(t):
                s, n = TILES[t]
                pe.wait_ge(lnT_ready, t + 1)
                if ROUTER_BANKS[t] == 0:
                    pe.wait_ge(h2_ready, 3)
                if ROUTER_BANKS[t] == 3:
                    pe.wait_ge(h2_ready, 5)
                dst = bank[ROUTER_BANKS[t]][0:n, LOGIT_COLS]
                for c in range(DC):
                    mm(dst, lnT_sb[:, c, s:s + n], rw_sb[:, c, :], start=c == 0, stop=False)
                mm(dst, ones[0:1, 0:n], rb_sb[:, :], start=False, stop=True).then_inc(router_mm, 1)

            def count(t):
                n = TILES[t][1]
                pe.wait_ge(logits_ready, t + 1)
                dst = bank[ROUTER_BANKS[t]][0:n, COUNT_COLS]
                if t:
                    pe.wait_ge(upto_ready, t)
                    mm(dst, ones_bf[:, 0:n], chosen_upto[:, t - 1, :], start=True, stop=False)
                mm(dst, upto_bf[0:n, 0:n], chosen[0:n, t, :], start=t == 0, stop=True).then_inc(count_mm, 1)

            def dispatch(t):
                n = TILES[t][1]
                pe.wait_ge(p_ready, t + 1)
                pe.wait_ge(x_lo_ready, t + 1)
                for c in range(DC):
                    for half in range(2):
                        for part in (x_hi, x_lo):
                            last = mm(bank[XE_BANKS[c][half]][:, 0:HALF_SLOTS], part[0:n, t, c * 128:(c + 1) * 128],
                                      p_sb[0:n, t, 4 * half:4 * half + 4, :].rearrange("p e c -> p (e c)"),
                                      start=t == 0 and part is x_hi, stop=t == NT - 1 and part is x_lo)
                last.then_inc(dispatch_mm, 1)

            def transpose_p(t, q):
                n = TILES[t][1]
                pe.wait_ge(p_ready, t + 1)
                if t or q:
                    pe.wait_ge(pT_ready, 2 * t + q)
                for k in range(4):
                    last = pe.transpose(bank[P_BANK][0:CAP, k * 128:k * 128 + n],
                                        p_sb[0:n, t, 4 * q + k, :].bitcast(f32), ident[0:n, 0:n])
                last.then_inc(p_T, 1)

            for step in range(NG + 2):
                if step == 0:
                    pe.wait_ge(bf_ready, 7)
                    pe.wait_ge(v_ready, 2 * len(AT))
                    pe.wait_ge(qk0_ready, EARLY)
                    pe.wait_ge(lnT_lo_ready, NT)
                    pe.wait_ge(wo_in, 16)
                if step == len(AT):
                    pe.wait_ge(qk1_ready, len(QK_UNITS) - EARLY)
                if step < NG:
                    scores(step)
                project_qk(late_unit(step, 0))
                if step in WO_AT:
                    project_out(WO_AT[step])
                if 1 <= step <= NG:
                    transpose_e(step - 1)
                project_qk(late_unit(step, 1))
                if step == NG + 1:
                    pe.wait_ge(eT_ready, 2 * NG)
                    transpose_ln(NT)
                if step >= 2:
                    weigh_v(step - 2)
                project_qk(late_unit(step, 2))
            transpose_ln(NT + 1)
            pe.wait_ge(router_in, 32)
            route(0)
            project_out(4)
            route(1)
            transpose_ln(NT + 2)
            count(0)
            route(2)
            transpose_ln(NT + 3)
            count(1)
            pe.wait_ge(oT_ready, NG)
            transpose_p(0, 0)
            route(3)
            transpose_ln(NT + 4)
            transpose_p(0, 1)
            count(2)
            transpose_p(1, 0)
            route(4)
            transpose_p(1, 1)
            pe.wait_ge(slot_ready, 3)
            pe.wait_ge(h2_ready, 4)
            dispatch(0)
            transpose_p(2, 0)
            count(3)
            dispatch(1)
            transpose_p(2, 1)
            count(4)
            dispatch(2)
            transpose_p(3, 0)
            dispatch(3)
            transpose_p(3, 1)
            dispatch(4)
            transpose_p(4, 0)
            pe.wait_ge(slot_ready, NT)
            pe.wait_ge(gate_lo_ready, 1)
            for half in range(2):
                for t, (s, n) in enumerate(TILES):
                    last = mm(bank[GATE_BANKS[half]][0:2 * EXPERTS, 0:HALF_SLOTS],
                              gate_parts[0:n, t, :, :].rearrange("p a e -> p (a e)"),
                              p_sb[0:n, t, 4 * half:4 * half + 4, :].rearrange("p e c -> p (e c)"),
                              start=t == 0, stop=t == NT - 1)
            last.then_inc(gate_mm, 1)
            transpose_p(4, 1)

            def up(e):
                pe.wait_ge(expert_in[e], 32)
                if e % 4 == 0:
                    pe.wait_ge(xe0_ready, e // 4 + 1)
                    pe.wait_ge(xe1_ready, 2)
                for q in range(2):
                    if e >= 1:
                        pe.wait_ge(gelu_ready, 8 * (e - 1) + 4 * (q + 1))
                    elif q == 1:
                        pe.wait_ge(gate_rows_ready, 2)
                    for k in range(4):
                        hc = 4 * q + k
                        for c in range(DC):
                            last = mm(bank[UP_BANKS[q]][:, k * CAP:(k + 1) * CAP], w1_sb[e][:, c, hc * 128:(hc + 1) * 128],
                                      xe_sb[:, c, e, :], start=c == 0, stop=c == DC - 1)
                    last.then_inc(up_mm, 1)

            def down(e):
                if e < 2:
                    pe.wait_ge(pT_ready, 2 * NT)
                if e >= 2:
                    pe.wait_ge(y_biased, e - 1)
                for c in range(HC):
                    pe.wait_ge(gelu_ready, 8 * e + c + 1)
                    last = mm(bank[DOWN_BANKS[e % 2]][0:CAP, 0:D], hidden_sb[:, e % 2, c, :], w2_sb[e][:, c, :],
                              start=c == 0, stop=c == HC - 1)
                last.then_inc(down_mm, 1)

            def combine(e):
                pe.wait_ge(y_ready, e + 1)
                if e == 0:
                    pe.wait_ge(xe0_ready, 2)
                for t, (s, n) in enumerate(TILES):
                    for part in (y_hi, y_lo):
                        last = mm(bank[t // 2][0:n, (t % 2) * D:(t % 2 + 1) * D], pT_sb[:, e, s:s + n], part[:, e % 2, :],
                                  start=e == 0 and part is y_hi and t % 2 == 0,
                                  stop=e == EXPERTS - 1 and part is y_lo and (t % 2 == 1 or t == NT - 1),
                                  skip_group_check=True)
                    if e == EXPERTS - 1 and (t % 2 == 1 or t == NT - 1):
                        last.then_inc(y_final, 1)
                if e < EXPERTS - 1:
                    last.then_inc(combine_mm, 1)

            up(0)
            for e in range(EXPERTS):
                last = pe.transpose(bank[GATE_T_BANK][0:CAP, e * 2 * EXPERTS:(e + 1) * 2 * EXPERTS], gate_rows[:, e, :],
                                    ident[0:2 * EXPERTS, 0:2 * EXPERTS])
            last.then_inc(gate_T, 1)
            up(1)
            down(0)
            for e in range(1, EXPERTS):
                if e + 1 < EXPERTS:
                    up(e + 1)
                down(e)
                combine(e - 1)
            combine(EXPERTS - 1)


def constants():
    import numpy as np

    c = np.zeros((128, C_END), np.float32)
    c[:, C_ID:C_ID + 128] = np.eye(128)
    c[:, C_TRI:C_TRI + 128] = np.triu(np.ones((128, 128)))
    c[:, C_ONE:C_ONE + 128] = 1.0
    c[:, C_SLOT:C_SLOT + CAP] = np.arange(1, CAP + 1)
    c[:, C_EXP:C_EXP + EXPERTS] = np.arange(EXPERTS)
    c[:, C_EPS] = EPS
    for i in range(PER):
        mine = slice(i * SEQ, (i + 1) * SEQ)
        for row in (i, 64 + i):
            c[row, C_ML:C_ML + W3][mine] = 1.0
            c[row, C_MR:C_MR + W3] = -BIG
            c[row, C_MR:C_MR + W3][mine] = 0.0
    sel = np.zeros((EMB_ROWS, IMAGES, SEQ), np.float32)
    for i in range(SEQ):
        sel[i, :, i] = 1.0
        sel[SEQ if i else SEQ + 1, :, i] = 1.0
    return c, sel.reshape(EMB_ROWS, TOKENS)


def kernel(x, L0_tok_W, L0_tok_b, L0_tok_class_token, L0_tok_pos_embedding, L0_attn_Wq, L0_attn_bq, L0_attn_Wk,
           L0_attn_bk, L0_attn_Wv, L0_attn_bv, L0_attn_Wo, L0_attn_bo, L0_ffn_router_w, L0_ffn_router_b, L0_ffn_w1,
           L0_ffn_b1, L0_ffn_w2, L0_ffn_b2):
    import numpy as np
    import concourse.bacc as bacc
    from concourse.bass_utils import run_bass_kernel_spmd

    p = np.asarray(x).reshape(IMAGES, CHANNELS, GRID, PATCH, GRID, PATCH).transpose(1, 3, 5, 0, 2, 4)
    cols = np.zeros((PATCH_IN, IMAGES, SEQ), np.float32)
    cols[:, :, 1:] = p.reshape(PATCH_IN, IMAGES, GRID * GRID)
    padded = np.zeros((PATCH_IN, NT * 128), np.float32)
    padded[:, :TOKENS] = cols.reshape(PATCH_IN, TOKENS)
    consts, sel = constants()
    arrays = {
        "patches": padded.reshape(PC, 128, NT, 128).transpose(1, 2, 0, 3),
        "wT": np.asarray(L0_tok_W).T.reshape(PC, 128, D).transpose(1, 0, 2),
        "emb": np.concatenate([np.asarray(L0_tok_pos_embedding)[0], np.asarray(L0_tok_b)[None],
                               np.asarray(L0_tok_class_token)[0]]),
        "emb_sel": sel, "consts": consts,
        "wq": L0_attn_Wq, "wk": L0_attn_Wk, "wv": L0_attn_Wv,
        "bqk": np.stack([np.asarray(L0_attn_bq), np.asarray(L0_attn_bk)]).reshape(2, PAIRS, 128).transpose(2, 0, 1),
        "bv": L0_attn_bv, "wo": L0_attn_Wo, "bo": L0_attn_bo, "rw": L0_ffn_router_w, "rb": L0_ffn_router_b,
        "w1": L0_ffn_w1, "b1": np.asarray(L0_ffn_b1).reshape(EXPERTS, HC, 128).transpose(2, 0, 1),
        "w2": L0_ffn_w2, "b2": L0_ffn_b2,
    }
    arrays = {k: np.ascontiguousarray(v) for k, v in arrays.items()}
    nc = bacc.Bacc("TRN2", target_bir_lowering=False, num_devices=1)
    args = [nc.dram_tensor(k, a.shape, mybir.dt.from_np(a.dtype), kind="ExternalInput").ap() for k, a in arrays.items()]
    out = nc.dram_tensor("out", (TOKENS, D), mybir.dt.float32, kind="ExternalOutput").ap()
    build(nc, *args, out)
    r = run_bass_kernel_spmd(nc, [arrays], core_ids=[0])
    return r.results[0]["out"].reshape(IMAGES, SEQ, D)
```

```python
from contextlib import ExitStack

import concourse.bass as bass
from concourse import mybir

IMAGES, CHANNELS, SIDE, PATCH = 16, 3, 96, 16
GRID = SIDE // PATCH
SEQ = GRID * GRID + 1
TOKENS = IMAGES * SEQ
D = 256
DC = D // 128
PATCH_IN = CHANNELS * PATCH * PATCH
PC = PATCH_IN // 128
HEADS, HD = 16, 64
PAIRS = HEADS * HD // 128
EXPERTS, HIDDEN = 8, 1024
HC = HIDDEN // 128
CAP = -(-TOKENS * 5 // (EXPERTS * 4))
SLOTS = EXPERTS * CAP
HALF_SLOTS = SLOTS // 2
EMB_ROWS = SEQ + 2
TILES = [(s, min(128, TOKENS - s)) for s in range(0, TOKENS, 128)]
NT = len(TILES)
PER = 3
AT = [(s, min(PER * SEQ, TOKENS - s)) for s in range(0, TOKENS, PER * SEQ)]
W3 = PER * SEQ
HALF = TOKENS // 2
EPS = 1e-5
BIG = 2.0 ** 126
WARM_UP = 9

C_ID, C_TRI, C_ONE, C_SLOT, C_EXP, C_ML, C_MR, C_EPS, C_END = 0, 128, 256, 384, 480, 488, 600, 712, 720


def build(nc, patches, wT, emb, emb_sel, consts, wq, wk, wv, bqk, bv, wo, bo, rw, rb, w1, b1, w2, b2, out):
    f32, f32r, bf16, u32 = mybir.dt.float32, mybir.dt.float32r, mybir.dt.bfloat16, mybir.dt.uint32
    ALU, ACT, AX = mybir.AluOpType, mybir.ActivationFunctionType, mybir.AxisListType
    ctx = ExitStack()
    with ctx:
        def sem(name):
            return ctx.enter_context(nc.semaphore(name))

        arena = ctx.enter_context(nc.sbuf_tensor("arena", [128, 212736 // 4], f32))
        base = nc.sbuf_base - 212736
        at = [base]

        def region(n_bytes):
            start = at[0]
            at[0] += -(-n_bytes // 32) * 32
            assert at[0] <= base + 212736
            return start

        def sb(name, shape, dt, offset=None):
            n_bytes = 2 if dt == bf16 else 4
            for n in shape[1:]:
                n_bytes *= n
            return nc.alloc_sbuf_tensor_at(name, shape, dt, offset=region(n_bytes) if offset is None else offset)

        EXPERT_BYTES = 4 * (DC * HIDDEN + HC * D)
        r_own = [region(EXPERT_BYTES), region(EXPERT_BYTES)]
        r_qkvw = region(4 * 3 * DC * 1024)
        r_patch = region(4 * (NT * PC * 128 + PC * D))
        r_v = region(4 * len(AT) * 1024)
        r_qk = region(4 * 2 * PAIRS * TOKENS)
        r_e = region(4 * 4 * 8 * W3)
        r_lnT = region(4 * DC * TOKENS)
        r_ot = region(4 * PAIRS * TOKENS)

        w_raw = sb("w_raw", [128, 3, DC, 1024], f32, r_own[0])
        w_hi = sb("w_hi", [128, 3, DC, 1024], f32r, r_qkvw)
        wqk_lo = [sb(f"wqk_lo{o}", [128, 2, DC, 512], f32r, r_ot + o * 4 * PAIRS // 2 * TOKENS) for o in range(2)]
        wv_lo = sb("wv_lo", [128, DC, 1024], f32r, r_e)
        lnT_hi = sb("lnT_hi", [128, DC, TOKENS], f32r, r_lnT)
        lnT_lo = sb("lnT_lo", [128, DC, TOKENS], f32r, r_own[0] + 2 * EXPERT_BYTES - 4 * DC * TOKENS)
        b2_sb = sb("b2_sb", [CAP, EXPERTS, D], f32, r_qkvw + EXPERT_BYTES)
        patches_sb = sb("patches_sb", [128, NT, PC, 128], f32, r_patch)
        wT_sb = sb("wT_sb", [128, PC, D], f32, r_patch + 4 * NT * PC * 128)
        v_sb = sb("v_sb", [W3, len(AT), 1024], f32, r_v)
        hidden_sb = sb("hidden_sb", [128, 2, HC, CAP], f32, r_v + EXPERT_BYTES)
        qT_sb = sb("qT_sb", [128, PAIRS, TOKENS], f32, r_qk)
        kT_sb = sb("kT_sb", [128, PAIRS, TOKENS], f32, r_qk + 4 * PAIRS * TOKENS)
        p_sb = sb("p_sb", [128, NT, EXPERTS, CAP], f32r, r_qk)
        pT_sb = sb("pT_sb", [CAP, EXPERTS, TOKENS], f32r, r_qk + 4 * PAIRS * TOKENS)
        e_sb = sb("e_sb", [W3, 2, 2, 4, W3], f32, r_e)
        eT_sb = sb("eT_sb", [W3, 2, 2, 4, W3], f32, r_e + 4 * 16 * W3)
        x_hi = sb("x_hi", [128, NT, D], f32r, r_e)
        x_lo = sb("x_lo", [128, NT, D], f32r, r_e + 4 * NT * D)
        oT_hi = sb("oT_hi", [128, PAIRS, TOKENS], f32r, r_ot)
        oT_lo = sb("oT_lo", [128, PAIRS, TOKENS], f32r, r_own[0])
        wo_hi = sb("wo_hi", [128, PAIRS, D], f32r, r_own[0] + 4 * PAIRS * TOKENS)
        xe_sb = sb("xe_sb", [128, DC, EXPERTS, CAP], f32, r_ot)
        y_at = r_ot + 4 * DC * SLOTS
        y_sb = sb("y_sb", [CAP, 2, D], f32, y_at)
        y_hi = sb("y_hi", [CAP, 2, D], f32r, y_at + 4 * 2 * D)
        y_lo = sb("y_lo", [CAP, 2, D], f32r, y_at + 4 * 4 * D)
        hidden_hi = sb("hidden_hi", [128, 2, HC, CAP], f32r, y_at + 4 * 6 * D)
        hidden_lo = sb("hidden_lo", [128, 2, HC, CAP], f32r, r_v + EXPERT_BYTES)

        slot_at = [r_patch, r_qkvw, r_v, r_own[0], r_own[1], r_patch, r_qkvw, r_v]
        w1_sb = [sb(f"w1_{e}", [128, DC, HIDDEN], f32, slot_at[e]) for e in range(EXPERTS)]
        w2_sb = [sb(f"w2_{e}", [128, HC, D], f32, slot_at[e] + 4 * DC * HIDDEN) for e in range(EXPERTS)]

        w2_lo = [sb(f"w2_lo{e}", [128, HC, D], f32r, slot_at[e] + 4 * DC * HIDDEN) for e in range(EXPERTS)]
        r_wo = region(4 * PAIRS * D)
        wo_sb = sb("wo_sb", [128, PAIRS, D], f32, r_wo)
        wo_lo = sb("wo_lo", [128, PAIRS, D], f32r, r_wo)
        w2_hi = [sb(f"w2_hi{i}", [128, HC, D], f32r, r) for i, r in enumerate((r_wo, r_e))]
        ones_bf = sb("ones_bf", [128, 128], bf16)
        upto_bf = sb("upto_bf", [128, 128], bf16)
        bv_sb = sb("bv_sb", [W3, 1024], f32)
        bo_sb = sb("bo_sb", [128, D], f32)
        h_sb = sb("h_sb", [128, NT, D], f32)
        ln_sb = sb("ln_sb", [128, 3, D], f32)
        lnT_sb = sb("lnT_sb", [128, DC, TOKENS], f32, r_lnT)
        const_sb = sb("const_sb", [128, C_END], f32)
        maskL = sb("maskL", [128, W3], bf16)
        maskR = sb("maskR", [128, 4, W3], bf16)
        emb_sb = sb("emb_sb", [EMB_ROWS, D], f32)
        sel_sb = sb("sel_sb", [EMB_ROWS, TOKENS], f32)
        bqk_sb = sb("bqk_sb", [128, 2, PAIRS], f32)
        rw_sb = sb("rw_sb", [128, DC, EXPERTS], f32)
        rb_sb = sb("rb_sb", [1, EXPERTS], f32)
        b1_sb = sb("b1_sb", [128, EXPERTS, HC], f32)
        stats = sb("stats", [128, 2 * NT, 6], f32)
        mean_var = sb("mean_var", [128, 2 * NT, 2], f32)
        std = sb("std", [128, 2 * NT], f32)
        rstd = sb("rstd", [128, 2 * NT], f32)
        neg_max = sb("neg_max", [W3, 2, 2, 4], f32)
        row_sum = sb("row_sum", [W3, 2, 2, 4], f32)
        row_inv = sb("row_inv", [W3, 2, 2, 4], f32)
        logits = sb("logits", [128, NT, EXPERTS], f32)
        top8 = sb("top8", [128, NT, 8], f32)
        top_at = sb("top_at", [128, NT, 8], u32)
        first = sb("first", [128, NT, EXPERTS], f32)
        chosen = sb("chosen", [128, NT, EXPERTS], bf16)
        chosen_upto = sb("chosen_upto", [128, NT, EXPERTS], bf16)
        slot = sb("slot", [128, NT, EXPERTS], f32)
        shifted = sb("shifted", [128, NT, EXPERTS], f32)
        gate_exp = sb("gate_exp", [128, NT, EXPERTS], f32)
        gate_sum = sb("gate_sum", [128, NT], f32)
        gate_inv = sb("gate_inv", [128, NT], f32)
        gates = sb("gates", [128, NT, EXPERTS], f32)
        gate_parts = sb("gate_parts", [128, NT, 2, EXPERTS], f32r)
        gate_rows = sb("gate_rows", [2 * EXPERTS, EXPERTS, CAP], f32, r_e + 4 * 2 * NT * D)
        warm = sb("warm", [1, 1], f32)
        zeros_bf = sb("zeros_bf", [128, 512], bf16, r_e)
        slot_gate_hi = sb("slot_gate_hi", [CAP, EXPERTS], f32)
        slot_gate = sb("slot_gate", [CAP, EXPERTS], f32)

        bank = [ctx.enter_context(nc.psum_tensor(f"bank{i}", [128, 512], f32)) for i in range(8)]

        ident = const_sb[:, C_ID:C_ID + 128]
        ones = const_sb[:, C_ONE:C_ONE + 128]
        slot_no = const_sb[:, C_SLOT:C_SLOT + CAP]
        expert_no = const_sb[:, C_EXP:C_EXP + EXPERTS]
        eps = const_sb[:, C_EPS:C_EPS + 1]

        def sems(names):
            return [sem(n) for n in names.split()]

        const_in, emb_in, bv_in, bqk_in, wo_in, bo_in, router_in, b1_in, b2_in = sems(
            "const_in emb_in bv_in bqk_in wo_in bo_in router_in b1_in b2_in")
        wT_in = [sem(f"wT_in{i}") for i in range(2)]
        patch0_in = [sem(f"patch0_in{i}") for i in range(2)]
        patches_in = [None] + [sem(f"patches_in{t}") for t in range(1, NT)]
        w_in = [sem(f"w_in{i}") for i in range(3)]
        expert_in = [sem(f"expert_in{e}") for e in range(EXPERTS)]
        out_sent = sem("out_sent")
        (patch_mm, ln_T, v_mm, qk_mm, scores_mm, e_T, pv_mm, wo_mm, router_mm, count_mm, dispatch_mm, gate_mm,
         gate_T, p_T, up_mm, down_mm, combine_mm, y_final) = sems(
            "patch_mm ln_T v_mm qk_mm scores_mm e_T pv_mm wo_mm router_mm count_mm dispatch_mm gate_mm "
            "gate_T p_T up_mm down_mm combine_mm y_final")
        warm_mm = sem("warm_mm")
        (h_ready, std_ready, lnT_hi_ready, lnT_ready, qk0_ready, exp_ready, oT_ready, pT_ready, gate_exp_ready,
         xe0_ready, gate_rows_ready, gelu_table, gelu_ready) = sems(
            "h_ready std_ready lnT_hi_ready lnT_ready qk0_ready exp_ready oT_ready pT_ready gate_exp_ready "
            "xe0_ready gate_rows_ready gelu_table gelu_ready")
        (zeros_ready, wo_hi_ready, oT_lo_ready, bf_ready, stats_ready, mv_ready, rstd_ready, ln_ready, lnT_lo_ready, w_hi_ready, v_ready, qk1_ready,
         max_ready, inv_ready, eT_ready, h2_ready, top_ready, top_at_ready, first_ready, chosen_ready, logits_ready,
         slot_ready, p_ready, shifted_ready, gate_sum_ready, gate_inv_ready, gates_ready, gate_hi_ready,
         gate_lo_ready, xe1_ready, slot_gate_hi_ready, slot_gate_ready, hidden_hi_ready, hidden_ready,
         y_biased, y_hi_ready, y_ready, out_ready) = sems(
            "zeros_ready wo_hi_ready oT_lo_ready bf_ready stats_ready mv_ready rstd_ready ln_ready lnT_lo_ready w_hi_ready v_ready qk1_ready "
            "max_ready inv_ready eT_ready h2_ready top_ready top_at_ready first_ready chosen_ready logits_ready "
            "slot_ready p_ready shifted_ready gate_sum_ready gate_inv_ready gates_ready gate_hi_ready "
            "gate_lo_ready xe1_ready slot_gate_hi_ready slot_gate_ready hidden_hi_ready hidden_ready "
            "y_biased y_hi_ready y_ready out_ready")
        zero_ready, w_lo_ready, hb_ready, norm_ready, x_hi_ready, x_lo_ready, upto_ready, w2_hi_ready, w2_lo_ready, wo_lo_ready = sems(
            "zero_ready w_lo_ready hb_ready norm_ready x_hi_ready x_lo_ready upto_ready w2_hi_ready w2_lo_ready wo_lo_ready")

        V_BANKS, QK_BANKS, LATE_QK_BANK = [0, 1, 2], [3, 4, 7], 7
        EMBED_BANKS = range(NT)
        E_BANKS, OUT_BANK = [4, 5], 6
        WO_BANKS = [7, 7, 0, 7, 3]
        LNT2_BANKS = [1, 5, 1, 5, 5]
        ROUTER_BANKS = [4, 2, 4, 3, 4]
        LOGIT_COLS, COUNT_COLS = slice(0, EXPERTS), slice(EXPERTS, 2 * EXPERTS)
        XE_BANKS = [[0, 1], [2, 7]]
        P_BANK, GATE_BANKS, GATE_T_BANK = 6, [3, 4], 3
        UP_BANKS, DOWN_BANKS = [7, 4], [5, 6]

        def lnT_bank(i):
            return bank[5 + i % 2 if i < NT else LNT2_BANKS[i - NT]]

        def score_bank(g, b):
            return bank[2 * (g % 2) + b]

        GROUPS = [(0, len(AT) - 1)] + [(0, a) for a in range(len(AT) - 1)] + [(1, a) for a in range(len(AT))]
        NG = len(GROUPS)
        QK_UNITS = [(pair, which, half) for pair in range(PAIRS) for which in range(2) for half in range(2)]
        EARLY = len(QK_UNITS) // 2 + 1
        LATE_PLACES = [(0, 1), (0, 2), (0, 1, 2), (0, 1, 2), (0, 1, 2), (0, 1)]
        LATE_AT = {}
        for s, places in enumerate(LATE_PLACES):
            for k in places:
                LATE_AT[s, k] = EARLY + len(LATE_AT)
        assert EARLY + len(LATE_AT) == len(QK_UNITS) and len(LATE_PLACES) == len(AT)
        WO_STEP = NG - 2
        W_PIECES = [(i, c, half) for i in (2, 0, 1) for c in range(DC) for half in range(2)]
        V_PIECES = 4
        WO_PIECES = 4

        OUT_PARTS = [(0, 2, 0, 128), (2, 2, 256, 128), (4, 1, TILES[4][0], TILES[4][1])]

        def late_unit(step, k):
            return LATE_AT.get((step, k))

        block = ctx.enter_context(nc.Block())

        @block.sync
        def _(sp):
            for i in range(2):
                cs = slice(i * PC // 2, (i + 1) * PC // 2)
                sp.dma_start(patches_sb[:, 0, cs, :], patches[:, 0, cs, :]).then_inc(patch0_in[i], 16)
            for t in range(1, NT):
                sp.dma_start(patches_sb[:, t, :, :], patches[:, t, :, :]).then_inc(patches_in[t], 16)
                if t == 1:
                    sp.dma_start(const_sb[:, :], consts).then_inc(const_in, 16)
            for i, w in ((2, wv), (0, wq), (1, wk)):
                sp.dma_start(w_raw[:, i, :, :], w.rearrange("(c p) n -> p c n", p=128)).then_inc(w_in[i], 16)
            sp.dma_start(wo_sb[:, :, :], wo.rearrange("(c p) n -> p c n", p=128)).then_inc(wo_in, 16)

            def load_expert(e):
                sp.dma_start(w1_sb[e][:, :, :], w1[e].rearrange("(c p) n -> p c n", p=128)).then_inc(expert_in[e], 16)
                sp.dma_start(w2_sb[e][:, :, :], w2[e].rearrange("(c p) n -> p c n", p=128)).then_inc(expert_in[e], 16)

            sp.wait_ge(patch_mm, NT)
            load_expert(0)
            sp.wait_ge(v_mm, 2 * len(AT))
            sp.wait_ge(qk_mm, len(QK_UNITS))
            load_expert(1)
            sp.dma_start(b2_sb[:, :, :], b2.unsqueeze(0).to_broadcast([CAP, EXPERTS, D])).then_inc(b2_in, 16)
            sp.wait_ge(pv_mm, NG)
            load_expert(2)
            sp.wait_ge(wo_mm, NT)
            load_expert(3)
            load_expert(4)
            for e, used in ((5, 0), (6, 1), (7, 2)):
                sp.wait_ge(down_mm, used + 1)
                load_expert(e)
            for i, (t, m, s, n) in enumerate(OUT_PARTS):
                sp.wait_ge(out_ready, i + 1)
                sp.dma_start(out[s:s + m * n, :].rearrange("(m p) n -> p m n", p=n), h_sb[0:n, t:t + m, :])\
                  .then_inc(out_sent, 16)
            sp.wait_ge(out_sent, 16 * len(OUT_PARTS))

        @block.gpsimd
        def _(pool):
            pool.memset(logits[:, :, :], 0.0).then_inc(zero_ready, 1)
            pool.memset(top8[:, :, :], 0.0).then_inc(zero_ready, 1)
            pool.wait_ge(const_in, 16)
            pool.dma_start(bv_sb[:, :], bv.unsqueeze(0).to_broadcast([W3, 1024])).then_inc(bv_in, 16)
            pool.dma_start(bqk_sb[:, :, :], bqk).then_inc(bqk_in, 16)
            pool.dma_start(bo_sb[:, :], bo.unsqueeze(0).to_broadcast([128, D])).then_inc(bo_in, 16)
            pool.dma_start(rw_sb[:, :, :], rw.rearrange("(c p) n -> p c n", p=128)).then_inc(router_in, 16)
            pool.dma_start(rb_sb[:, :], rb.unsqueeze(0)).then_inc(router_in, 16)
            pool.dma_start(b1_sb[:, :, :], b1).then_inc(b1_in, 16)
            for k, (i, c, half) in enumerate(W_PIECES):
                cols = slice(half * 512, (half + 1) * 512)
                pool.wait_ge(w_hi_ready, k + 1)
                if k == 0:
                    pool.wait_ge(warm_mm, 1)
                lo = wv_lo[:, c, cols] if i == 2 else wqk_lo[half][:, i, c, :]
                pool.tensor_tensor(lo, w_raw[:, i, c, cols], w_hi[:, i, c, cols].bitcast(f32), ALU.subtract)\
                    .then_inc(w_lo_ready, 1)
            for k in range(WO_PIECES):
                cs = slice(k * PAIRS // WO_PIECES, (k + 1) * PAIRS // WO_PIECES)
                pool.wait_ge(wo_hi_ready, k + 1)
                pool.tensor_tensor(wo_lo[:, cs, :], wo_sb[:, cs, :], wo_hi[:, cs, :].bitcast(f32),
                                   ALU.subtract).then_inc(wo_lo_ready, 1)
            pool.wait_ge(bo_in, 16)
            for t, (s, n) in enumerate(TILES):
                pool.wait_ge(ln_ready, t + 1)
                pool.tensor_tensor(h_sb[0:n, t, :], h_sb[0:n, t, :], bo_sb[0:n, :], ALU.add).then_inc(hb_ready, 1)
            for g, (o, a) in enumerate(GROUPS):
                n = AT[a][1]
                for b in range(2):
                    pool.wait_ge(inv_ready, 2 * g + b + 1)
                    e = e_sb[0:n, g % 2, b, :, 0:n]
                    pool.tensor_tensor(e, e, row_inv[0:n, g % 2, b, :].unsqueeze(2).to_broadcast([n, 4, n]),
                                       ALU.mult).then_inc(norm_ready, 1)

            def low_x(t):
                n = TILES[t][1]
                pool.wait_ge(x_hi_ready, t + 1)
                pool.tensor_tensor(x_lo[0:n, t, :], ln_sb[0:n, (NT + t) % 3, :], x_hi[0:n, t, :].bitcast(f32),
                                   ALU.subtract).then_inc(x_lo_ready, 1)

            def sum_chosen(t):
                n = TILES[t][1]
                pool.wait_ge(chosen_ready, t + 1)
                if t == 0:
                    pool.tensor_copy(chosen_upto[:, 0, :], chosen[:, 0, :]).then_inc(upto_ready, 1)
                else:
                    pool.wait_ge(upto_ready, t)
                    pool.tensor_tensor(chosen_upto[:, t, :], chosen_upto[:, t - 1, :], chosen[:, t, :],
                                       ALU.add).then_inc(upto_ready, 1)

            low_x(0)
            low_x(1)
            sum_chosen(0)
            low_x(2)
            sum_chosen(1)
            low_x(3)
            sum_chosen(2)
            low_x(4)
            sum_chosen(3)
            for e in range(EXPERTS):
                for k in range(2):
                    cs = slice(k * HC // 2, (k + 1) * HC // 2)
                    pool.wait_ge(w2_hi_ready, 2 * e + k + 1)
                    pool.tensor_tensor(w2_lo[e][:, cs, :], w2_sb[e][:, cs, :], w2_hi[e % 2][:, cs, :].bitcast(f32),
                                       ALU.subtract).then_inc(w2_lo_ready, 1)

        @block.scalar
        def _(act):
            for i in range(2):
                cs = slice(i * PC // 2, (i + 1) * PC // 2)
                act.dma_start(wT_sb[:, cs, :], wT[:, cs, :]).then_inc(wT_in[i], 16)
            act.dma_start(emb_sb[:, :], emb).then_inc(emb_in, 16)
            act.dma_start(sel_sb[:, :], emb_sel).then_inc(emb_in, 16)

            def std_of(i):
                n = TILES[i % NT][1]
                act.wait_ge(mv_ready, i + 1)
                act.activation(std[0:n, i:i + 1], mean_var[0:n, i, 1:2], ACT.Sqrt, bias=eps[0:n, :]).then_inc(std_ready, 1)

            def copy_lnT(i):
                s, n = TILES[i % NT]
                act.wait_ge(ln_T, i + 1)
                src = lnT_bank(i)[:, 0:D].rearrange("p (c n) -> p c n", c=DC)[:, :, 0:n]
                if i < NT:
                    act.activation(lnT_hi[:, :, s:s + n], src, ACT.Copy).then_inc(lnT_hi_ready, 1)
                else:
                    act.activation(lnT_sb[:, :, s:s + n], src, ACT.Copy).then_inc(lnT_ready, 1)

            act.wait_ge(const_in, 16)
            for t, (s, n) in enumerate(TILES):
                act.wait_ge(patch_mm, t + 1)
                act.activation(h_sb[0:n, t, :], bank[EMBED_BANKS[t]][0:n, 0:D], ACT.Copy).then_inc(h_ready, 1)
                std_of(t)
                if t >= 2:
                    copy_lnT(t - 2)
            copy_lnT(NT - 2)
            copy_lnT(NT - 1)
            act.wait_ge(bqk_in, 16)
            for u in range(EARLY):
                pair, which, half = QK_UNITS[u]
                act.wait_ge(qk_mm, u + 1)
                act.activation((qT_sb, kT_sb)[which][:, pair, half * HALF:(half + 1) * HALF],
                               bank[QK_BANKS[u % 3]][:, 0:HALF], ACT.Identity,
                               bias=bqk_sb[:, which, pair:pair + 1]).then_inc(qk0_ready, 1)

            def exps(g, b):
                n = AT[GROUPS[g][1]][1]
                if g >= 2 and b == 0:
                    act.wait_ge(e_T, 2 * (g - 1))
                act.wait_ge(max_ready, 2 * g + b + 1)
                for j in range(4):
                    act.activation(e_sb[0:n, g % 2, b, j, 0:n], score_bank(g, b)[0:n, j * W3:j * W3 + n], ACT.Exp,
                                   bias=neg_max[0:n, g % 2, b, j:j + 1],
                                   accum_out=row_sum[0:n, g % 2, b, j:j + 1]).then_inc(exp_ready, 1)

            def copy_oT(g):
                o, a = GROUPS[g]
                s, n = AT[a]
                act.wait_ge(pv_mm, g + 1)
                act.activation(oT_hi[:, 4 * o:4 * o + 4, s:s + n],
                               bank[OUT_BANK][:, 0:4 * W3].rearrange("p (j n) -> p j n", j=4)[:, :, 0:n],
                               ACT.Copy).then_inc(oT_ready, 1)

            for step in range(NG):
                exps(step, 0)
                if 2 <= step < WO_STEP:
                    copy_oT(step - 2)
                exps(step, 1)
                if step >= WO_STEP:
                    copy_oT(step - 2)

            def high_x(t):
                n = TILES[t][1]
                act.wait_ge(ln_ready, NT + t + 1)
                act.activation(x_hi[0:n, t, :], ln_sb[0:n, (NT + t) % 3, :], ACT.Copy).then_inc(x_hi_ready, 1)

            std_of(NT)
            std_of(NT + 1)
            copy_oT(NG - 2)
            copy_lnT(NT)
            copy_lnT(NT + 1)
            copy_oT(NG - 1)
            std_of(NT + 2)
            act.wait_ge(e_T, 2 * NG)
            high_x(0)
            high_x(1)
            copy_lnT(NT + 2)
            std_of(NT + 3)
            high_x(2)
            copy_lnT(NT + 3)

            def high_w2(e):
                act.wait_ge(expert_in[e], 32)
                if e == 0:
                    act.wait_ge(wo_mm, NT)
                elif e == 1:
                    act.wait_ge(dispatch_mm, NT)
                    act.wait_ge(x_lo_ready, NT)
                else:
                    act.wait_ge(down_mm, e - 1)
                for k in range(2):
                    cs = slice(k * HC // 2, (k + 1) * HC // 2)
                    act.activation(w2_hi[e % 2][:, cs, :], w2_sb[e][:, cs, :], ACT.Copy).then_inc(w2_hi_ready, 1)

            def copy_pT(t, q):
                s, n = TILES[t]
                act.wait_ge(p_T, 2 * t + q + 1)
                act.activation(pT_sb[:, 4 * q:4 * q + 4, s:s + n],
                               bank[P_BANK][0:CAP, :].rearrange("p (e n) -> p e n", e=4)[:, :, 0:n],
                               ACT.Copy).then_inc(pT_ready, 1)

            copy_pT(0, 0)
            high_x(3)
            std_of(NT + 4)
            copy_pT(0, 1)
            high_w2(0)
            copy_lnT(NT + 4)
            high_x(4)
            for t, q in ((1, 0), (1, 1), (2, 0)):
                copy_pT(t, q)
            act.wait_ge(shifted_ready, 1)
            act.activation(gate_exp[:, :, :], shifted[:, :, :], ACT.Exp).then_inc(gate_exp_ready, 1)
            act.wait_ge(b1_in, 16)
            act.activation(warm[:, :], b1_sb[0:1, 0, 0:1], ACT.Gelu).then_inc(gelu_table, 1)
            copy_pT(2, 1)
            act.wait_ge(dispatch_mm, NT)
            for half in range(2):
                act.activation(xe_sb[:, 0, 4 * half:4 * half + 4, :],
                               bank[XE_BANKS[0][half]][:, 0:HALF_SLOTS].rearrange("p (e c) -> p e c", e=4),
                               ACT.Copy).then_inc(xe0_ready, 1)
            act.wait_ge(gate_mm, 1)
            for half in range(2):
                act.activation(gate_rows[:, 4 * half:4 * half + 4, :],
                               bank[GATE_BANKS[half]][0:2 * EXPERTS, 0:HALF_SLOTS].rearrange("p (e c) -> p e c", e=4),
                               ACT.Copy).then_inc(gate_rows_ready, 1)
            copy_pT(3, 0)

            for e in range(EXPERTS):
                if e >= 2:
                    act.wait_ge(down_mm, e - 1)
                for q in range(2):
                    act.wait_ge(up_mm, 2 * e + q + 1)
                    for k in range(4):
                        c = 4 * q + k
                        act.activation(hidden_sb[:, e % 2, c, :], bank[UP_BANKS[q]][:, k * CAP:(k + 1) * CAP],
                                       ACT.Gelu, bias=b1_sb[:, e, c:c + 1]).then_inc(gelu_ready, 1)
                if e == 0:
                    copy_pT(3, 1)
                elif e == 1:
                    copy_pT(4, 0)
                    copy_pT(4, 1)
                if e + 1 < EXPERTS:
                    high_w2(e + 1)

        @block.vector
        def _(dve):
            def moments(i):
                t = i % NT
                n = TILES[t][1]
                dve.bn_stats(stats[0:n, i, :], h_sb[0:n, t, :]).then_inc(stats_ready, 1)
                dve.wait_ge(stats_ready, i + 1)
                dve.bn_aggr(mean_var[0:n, i, :], stats[0:n, i, :]).then_inc(mv_ready, 1)

            def normalise(i):
                t = i % NT
                n = TILES[t][1]
                dve.wait_ge(std_ready, i + 1)
                dve.reciprocal(rstd[0:n, i:i + 1], std[0:n, i:i + 1]).then_inc(rstd_ready, 1)
                dve.wait_ge(rstd_ready, i + 1)
                if i >= 3:
                    dve.wait_ge(ln_T, i - 2)
                if i >= NT + 3:
                    dve.wait_ge(x_lo_ready, i - NT - 2)
                dve.tensor_scalar(ln_sb[0:n, i % 3, :], h_sb[0:n, t, :], mean_var[0:n, i, 0:1],
                                  rstd[0:n, i:i + 1], ALU.subtract, ALU.mult).then_inc(ln_ready, 1)

            def lnT_low(t):
                s, n = TILES[t]
                dve.wait_ge(lnT_hi_ready, t + 1)
                dve.tensor_tensor(lnT_lo[:, :, s:s + n],
                                  lnT_bank(t)[:, 0:D].rearrange("p (c n) -> p c n", c=DC)[:, :, 0:n],
                                  lnT_hi[:, :, s:s + n].bitcast(f32), ALU.subtract).then_inc(lnT_lo_ready, 1)

            def weight_high(k):
                i, c, half = W_PIECES[k]
                cols = slice(half * 512, (half + 1) * 512)
                dve.wait_ge(w_in[i], 16)
                dve.tensor_copy(w_hi[:, i, c, cols], w_raw[:, i, c, cols]).then_inc(w_hi_ready, 1)

            dve.memset(zeros_bf[:, :], 0.0).then_inc(zeros_ready, 1)
            for t in range(NT):
                if t == 2:
                    for k in range(V_PIECES):
                        weight_high(k)
                dve.wait_ge(h_ready, t + 1)
                moments(t)
                if t >= 2:
                    lnT_low(t - 2)
                normalise(t)
            lnT_low(NT - 2)
            dve.wait_ge(bv_in, 16)
            for u in range(2 * len(AT)):
                a, half = u // 2, u % 2
                n = AT[a][1]
                if V_PIECES + u < len(W_PIECES):
                    weight_high(V_PIECES + u)
                dve.wait_ge(v_mm, u + 1)
                dve.tensor_tensor(v_sb[0:n, a, half * 512:(half + 1) * 512], bank[V_BANKS[u % 3]][0:n, :],
                                  bv_sb[0:n, half * 512:(half + 1) * 512], ALU.add).then_inc(v_ready, 1)
                if u == 1:
                    lnT_low(NT - 1)
                if u == 3:
                    dve.wait_ge(const_in, 16)
                    for j in range(4):
                        dve.tensor_copy(maskR[:, j, :], const_sb[:, C_MR:C_MR + W3]).then_inc(bf_ready, 1)
                    dve.tensor_copy(maskL[:, :], const_sb[:, C_ML:C_ML + W3]).then_inc(bf_ready, 1)
                    dve.tensor_copy(ones_bf[:, :], ones).then_inc(bf_ready, 1)
                    dve.tensor_copy(upto_bf[:, :], const_sb[:, C_TRI:C_TRI + 128]).then_inc(bf_ready, 1)

            dve.wait_ge(wo_in, 16)
            dve.wait_ge(w_lo_ready, len(W_PIECES))
            for k in range(WO_PIECES):
                cs = slice(k * PAIRS // WO_PIECES, (k + 1) * PAIRS // WO_PIECES)
                dve.tensor_copy(wo_hi[:, cs, :], wo_sb[:, cs, :]).then_inc(wo_hi_ready, 1)

            def row_max(g, b):
                n = AT[GROUPS[g][1]][1]
                dve.wait_ge(scores_mm, 2 * g + b + 1)
                if g >= 2:
                    dve.wait_ge(exp_ready, 8 * (g - 2) + 4 * (b + 1))
                dve.tensor_reduce(neg_max[0:n, g % 2, b, :],
                                  score_bank(g, b)[0:n, 0:4 * W3].rearrange("p (j n) -> p j n", j=4)[:, :, 0:n],
                                  AX.X, ALU.max, negate=True).then_inc(max_ready, 1)

            def copy_eT(g):
                n = AT[GROUPS[g][1]][1]
                if g >= 2:
                    dve.wait_ge(pv_mm, g - 1)
                for b in range(2):
                    dve.wait_ge(e_T, 2 * g + b + 1)
                    dve.tensor_copy(eT_sb[0:n, g % 2, b, :, 0:n],
                                    bank[E_BANKS[b]][0:n, 0:4 * W3].rearrange("p (j n) -> p j n", j=4)[:, :, 0:n])\
                       .then_inc(eT_ready, 1)

            def inverse_sums(g, b):
                n = AT[GROUPS[g][1]][1]
                dve.wait_ge(exp_ready, 8 * g + 4 * (b + 1))
                if g >= 2:
                    dve.wait_ge(norm_ready, 2 * (g - 2) + b + 1)
                dve.reciprocal(row_inv[0:n, g % 2, b, :], row_sum[0:n, g % 2, b, :]).then_inc(inv_ready, 1)

            def low_oT(g):
                o, a = GROUPS[g]
                s, n = AT[a]
                dve.wait_ge(oT_ready, g + 1)
                dve.tensor_tensor(oT_lo[:, 4 * o:4 * o + 4, s:s + n],
                                  bank[OUT_BANK][:, 0:4 * W3].rearrange("p (j n) -> p j n", j=4)[:, :, 0:n],
                                  oT_hi[:, 4 * o:4 * o + 4, s:s + n].bitcast(f32), ALU.subtract).then_inc(oT_lo_ready, 1)

            def late_qk(u):
                if u is not None:
                    pair, which, half = QK_UNITS[u]
                    dve.wait_ge(qk_mm, u + 1)
                    dve.tensor_scalar((qT_sb, kT_sb)[which][:, pair, half * HALF:(half + 1) * HALF],
                                      bank[LATE_QK_BANK][:, 0:HALF], bqk_sb[:, which, pair:pair + 1], None,
                                      ALU.add).then_inc(qk1_ready, 1)

            def residual(t):
                s, n = TILES[t]
                dve.wait_ge(wo_mm, t + 1)
                dve.wait_ge(hb_ready, t + 1)
                dve.tensor_tensor(h_sb[0:n, t, :], h_sb[0:n, t, :], bank[WO_BANKS[t]][0:n, 0:D], ALU.add)\
                   .then_inc(h2_ready, 1)
                dve.wait_ge(h2_ready, t + 1)
                moments(NT + t)

            dve.wait_ge(bqk_in, 16)
            for step in range(NG):
                if step == 0:
                    late_qk(late_unit(0, 0))
                row_max(step, 0)
                if step:
                    late_qk(late_unit(step, 0))
                row_max(step, 1)
                if step < WO_STEP:
                    late_qk(late_unit(step, 1))
                    if step >= 1:
                        copy_eT(step - 1)
                    inverse_sums(step, 0)
                    if step >= 2:
                        low_oT(step - 2)
                    inverse_sums(step, 1)
                    late_qk(late_unit(step, 2))
                elif step == WO_STEP:
                    inverse_sums(step, 0)
                    inverse_sums(step, 1)
                    copy_eT(step - 1)
                    low_oT(step - 2)
                else:
                    residual(0)
                    copy_eT(step - 1)
                    inverse_sums(step, 0)
                    inverse_sums(step, 1)
                    low_oT(step - 2)
            normalise(NT)
            residual(1)
            copy_eT(NG - 1)
            normalise(NT + 1)
            low_oT(NG - 2)
            residual(2)
            low_oT(NG - 1)
            normalise(NT + 2)

            def choose(t):
                n = TILES[t][1]
                now = bank[ROUTER_BANKS[t]][0:n, LOGIT_COLS]
                dve.wait_ge(router_mm, t + 1)
                dve.max(top8[0:n, t, :], now).then_inc(top_ready, 1)
                dve.wait_ge(top_ready, t + 1)
                dve.max_index(top_at[0:n, t, :], top8[0:n, t, :], now).then_inc(top_at_ready, 1)
                dve.wait_ge(top_at_ready, t + 1)
                dve.tensor_scalar(first[0:n, t, :], expert_no[0:n, :], top_at[0:n, t, 0:1], None,
                                  ALU.is_equal).then_inc(first_ready, 1)
                dve.wait_ge(first_ready, t + 1)
                dve.scalar_tensor_tensor(chosen[0:n, t, :], expert_no[0:n, :], top_at[0:n, t, 1:2],
                                         first[0:n, t, :], ALU.is_equal, ALU.add).then_inc(chosen_ready, 1)
                dve.tensor_copy(logits[0:n, t, :], now).then_inc(logits_ready, 1)

            def place(t):
                n = TILES[t][1]
                dve.wait_ge(count_mm, t + 1)
                dve.wait_ge(chosen_ready, t + 1)
                dve.tensor_tensor(slot[0:n, t, :], bank[ROUTER_BANKS[t]][0:n, COUNT_COLS], chosen[0:n, t, :],
                                  ALU.mult).then_inc(slot_ready, 1)
                dve.wait_ge(slot_ready, t + 1)
                dve.tensor_tensor(p_sb[0:n, t, :, :], slot_no[0:n, :].unsqueeze(1).to_broadcast([n, EXPERTS, CAP]),
                                  slot[0:n, t, :].unsqueeze(2).to_broadcast([n, EXPERTS, CAP]),
                                  ALU.is_equal).then_inc(p_ready, 1)

            dve.wait_ge(zero_ready, 2)
            choose(0)
            residual(3)
            choose(1)
            normalise(NT + 3)
            place(0)
            residual(4)
            choose(2)
            normalise(NT + 4)
            place(1)
            choose(3)
            place(2)
            place(3)
            choose(4)
            dve.wait_ge(logits_ready, NT)
            dve.tensor_tensor(shifted[:, :, :], logits[:, :, :], top8[:, :, 0:1].to_broadcast([128, NT, EXPERTS]),
                              ALU.subtract).then_inc(shifted_ready, 1)
            place(4)
            dve.wait_ge(gate_exp_ready, 1)
            dve.tensor_reduce(gate_sum[:, :], gate_exp[:, :, :], AX.X, ALU.add).then_inc(gate_sum_ready, 1)
            dve.wait_ge(gate_sum_ready, 1)
            dve.reciprocal(gate_inv[:, :], gate_sum[:, :]).then_inc(gate_inv_ready, 1)
            dve.wait_ge(gate_inv_ready, 1)
            dve.tensor_tensor(gates[:, :, :], gate_exp[:, :, :],
                              gate_inv[:, :].unsqueeze(2).to_broadcast([128, NT, EXPERTS]), ALU.mult).then_inc(gates_ready, 1)
            dve.wait_ge(gates_ready, 1)
            dve.tensor_copy(gate_parts[:, :, 0, :], gates[:, :, :]).then_inc(gate_hi_ready, 1)
            dve.wait_ge(gate_hi_ready, 1)
            dve.tensor_tensor(gate_parts[:, :, 1, :], gates[:, :, :], gate_parts[:, :, 0, :].bitcast(f32),
                              ALU.subtract).then_inc(gate_lo_ready, 1)

            dve.wait_ge(dispatch_mm, NT)
            for half in range(2):
                dve.tensor_copy(xe_sb[:, 1, 4 * half:4 * half + 4, :],
                                bank[XE_BANKS[1][half]][:, 0:HALF_SLOTS].rearrange("p (e c) -> p e c", e=4))\
                   .then_inc(xe1_ready, 1)
            dve.wait_ge(gate_T, 1)
            picked = bank[GATE_T_BANK][0:CAP, 0:EXPERTS * 2 * EXPERTS]
            step_e = 2 * EXPERTS + 1
            dve.tensor_copy(slot_gate_hi[:, :], picked[:, 0::step_e]).then_inc(slot_gate_hi_ready, 1)
            dve.wait_ge(slot_gate_hi_ready, 1)
            dve.tensor_tensor(slot_gate[:, :], slot_gate_hi[:, :], picked[:, EXPERTS::step_e], ALU.add)\
               .then_inc(slot_gate_ready, 1)

            dve.wait_ge(slot_gate_ready, 1)
            dve.wait_ge(b2_in, 16)
            def split_hidden(e):
                for q in range(2):
                    cs = slice(q * HC // 2, (q + 1) * HC // 2)
                    dve.wait_ge(gelu_ready, 8 * e + 4 * (q + 1))
                    dve.tensor_copy(hidden_hi[:, e % 2, cs, :], hidden_sb[:, e % 2, cs, :]).then_inc(hidden_hi_ready, 1)
                    dve.wait_ge(hidden_hi_ready, 2 * e + q + 1)
                    dve.tensor_tensor(hidden_lo[:, e % 2, cs, :], hidden_sb[:, e % 2, cs, :],
                                      hidden_hi[:, e % 2, cs, :].bitcast(f32), ALU.subtract).then_inc(hidden_ready, 1)

            split_hidden(0)
            for e in range(EXPERTS):
                if e + 1 < EXPERTS:
                    split_hidden(e + 1)
                dve.wait_ge(down_mm, e + 1)
                if e >= 2:
                    dve.wait_ge(y_ready, e - 1)
                dve.tensor_tensor(y_sb[:, e % 2, :], bank[DOWN_BANKS[e % 2]][0:CAP, 0:D], b2_sb[:, e, :],
                                  ALU.add).then_inc(y_biased, 1)
                dve.wait_ge(y_biased, e + 1)
                if e >= 2:
                    dve.wait_ge(combine_mm, e - 1)
                dve.tensor_scalar(y_hi[:, e % 2, :], y_sb[:, e % 2, :], slot_gate[:, e:e + 1], None,
                                  ALU.mult).then_inc(y_hi_ready, 1)
                dve.wait_ge(y_hi_ready, e + 1)
                dve.scalar_tensor_tensor(y_lo[:, e % 2, :], y_sb[:, e % 2, :], slot_gate[:, e:e + 1],
                                         y_hi[:, e % 2, :].bitcast(f32), ALU.mult, ALU.subtract).then_inc(y_ready, 1)
            for i, (t, m, s, n) in enumerate(OUT_PARTS):
                dve.wait_ge(y_final, i + 1)
                dve.tensor_tensor(h_sb[0:n, t:t + m, :], h_sb[0:n, t:t + m, :],
                                  bank[i][0:n, 0:m * D].rearrange("p (m n) -> p m n", m=m), ALU.add)\
                   .then_inc(out_ready, 1)

        @block.tensor
        def _(pe):
            mm = pe.matmul

            def embed(t):
                s, n = TILES[t]
                dst = bank[EMBED_BANKS[t]][0:n, 0:D]
                if t:
                    pe.wait_ge(patches_in[t], 16)
                for c in range(PC):
                    if t == 0 and c % (PC // 2) == 0:
                        pe.wait_ge(patch0_in[c // (PC // 2)], 16)
                        pe.wait_ge(wT_in[c // (PC // 2)], 16)
                    mm(dst, patches_sb[:, t, c, 0:n], wT_sb[:, c, :], start=c == 0, stop=False)
                if t == 0:
                    pe.wait_ge(emb_in, 32)
                mm(dst, sel_sb[:, s:s + n], emb_sb[:, :], start=False, stop=True).then_inc(patch_mm, 1)

            def transpose_ln(i):
                t = i % NT
                n = TILES[t][1]
                pe.wait_ge(ln_ready, i + 1)
                if 2 <= i < NT:
                    pe.wait_ge(lnT_lo_ready, i - 1)
                if i == NT:
                    pe.wait_ge(exp_ready, 8 * (NG - 1))
                elif i == NT + 1:
                    pe.wait_ge(eT_ready, 2 * NG)
                elif i > NT + 1:
                    pe.wait_ge(lnT_ready, i - NT - 1 if i < 2 * NT - 1 else i - NT)
                for c in range(DC):
                    last = pe.transpose(lnT_bank(i)[:, c * 128:c * 128 + n], ln_sb[0:n, i % 3, c * 128:(c + 1) * 128],
                                        ident[0:n, 0:n])
                last.then_inc(ln_T, 1)

            def project_v(a):
                s, n = AT[a]
                pe.wait_ge(lnT_lo_ready, (s + n - 1) // 128 + 1)
                for half in range(2):
                    u = 2 * a + half
                    cols = slice(half * 512, (half + 1) * 512)
                    if u >= 3:
                        pe.wait_ge(v_ready, u - 2)
                    for c in range(DC):
                        parts = ((lnT_hi, w_hi[:, 2, c, cols]), (lnT_hi, wv_lo[:, c, cols]), (lnT_lo, w_hi[:, 2, c, cols]))
                        for k, (x, w) in enumerate(parts):
                            last = mm(bank[V_BANKS[u % 3]][0:n, :], x[:, c, s:s + n], w,
                                      start=c == 0 and k == 0, stop=c == DC - 1 and k == 2)
                    last.then_inc(v_mm, 1)

            def project_qk(u):
                if u is None:
                    return
                pair, which, half = QK_UNITS[u]
                if u < EARLY:
                    dst = bank[QK_BANKS[u % 3]][:, 0:HALF]
                    if u >= 3:
                        pe.wait_ge(qk0_ready, u - 2)
                else:
                    dst = bank[LATE_QK_BANK][:, 0:HALF]
                    if u == EARLY:
                        pe.wait_ge(qk0_ready, EARLY - 1)
                    else:
                        pe.wait_ge(qk1_ready, u - EARLY)
                tokens, rows = slice(half * HALF, (half + 1) * HALF), slice(pair * 128, (pair + 1) * 128)
                lo_rows = slice(pair % 4 * 128, (pair % 4 + 1) * 128)
                for c in range(DC):
                    hi, lo = w_hi[:, which, c, rows], wqk_lo[pair // 4][:, which, c, lo_rows]
                    for k, (w, x) in enumerate(((hi, lnT_hi), (hi, lnT_lo), (lo, lnT_hi))):
                        last = mm(dst, w, x[:, c, tokens], start=c == 0 and k == 0, stop=c == DC - 1 and k == 2)
                last.then_inc(qk_mm, 1)

            pe.wait_ge(zeros_ready, 1)
            for _ in range(WARM_UP):
                last = mm(bank[7][:, :], zeros_bf[:, 0:128], zeros_bf[:, :], start=True, stop=True)
            last.then_inc(warm_mm, 1)

            embed(0)
            pe.wait_ge(const_in, 16)
            for t in range(1, NT):
                embed(t)
                if t >= 2:
                    transpose_ln(t - 2)
            transpose_ln(NT - 2)
            pe.wait_ge(w_lo_ready, V_PIECES)
            pe.wait_ge(h_ready, NT)
            project_v(0)
            transpose_ln(NT - 1)
            for a in range(1, len(AT)):
                project_v(a)
            pe.wait_ge(w_lo_ready, len(W_PIECES))
            for u in range(EARLY):
                project_qk(u)

            def scores(g):
                o, a = GROUPS[g]
                s, n = AT[a]
                masked = n > SEQ
                both = [slice(0, 64), slice(64, 128)]
                for b, rows in enumerate(both):
                    if g >= 2:
                        pe.wait_ge(exp_ready, 8 * (g - 2) + 4 * (b + 1))
                    if masked:
                        mm(score_bank(g, b)[0:n, 0:4 * W3], maskL[rows, :], maskR[rows, :, :].rearrange("p j n -> p (j n)"),
                           start=True, stop=False)
                for j in range(4):
                    for b, rows in enumerate(both):
                        last = mm(score_bank(g, b)[0:n, j * W3:j * W3 + n], qT_sb[rows, 4 * o + j, s:s + n],
                                  kT_sb[rows, 4 * o + j, s:s + n], start=not masked, stop=j == 3 or not masked)
                        if j == 3:
                            last.then_inc(scores_mm, 1)

            def transpose_e(g):
                n = AT[GROUPS[g][1]][1]
                for b in range(2):
                    pe.wait_ge(norm_ready, 2 * g + b + 1)
                    if g >= 1:
                        pe.wait_ge(eT_ready, 2 * (g - 1) + b + 1)
                    for j in range(4):
                        last = pe.transpose(bank[E_BANKS[b]][0:n, j * W3:j * W3 + n], e_sb[0:n, g % 2, b, j, 0:n],
                                            ident[0:n, 0:n])
                    last.then_inc(e_T, 1)

            def weigh_v(g):
                o, a = GROUPS[g]
                n = AT[a][1]
                pe.wait_ge(eT_ready, 2 * g + 2)
                if g >= 1:
                    pe.wait_ge(oT_lo_ready, g)
                for j in range(4):
                    for b in range(2):
                        head = 2 * (4 * o + j) + b
                        last = mm(bank[OUT_BANK][64 * b:64 * b + 64, j * W3:j * W3 + n],
                                  v_sb[0:n, a, head * HD:(head + 1) * HD], eT_sb[0:n, g % 2, b, j, 0:n],
                                  start=True, stop=True)
                last.then_inc(pv_mm, 1)

            def project_out(t):
                s, n = TILES[t]
                pe.wait_ge(oT_lo_ready, len(AT) + (s + n - 1) // W3 + 1)
                if WO_BANKS[t] == 7:
                    if t == 0:
                        pe.wait_ge(qk1_ready, len(QK_UNITS) - EARLY)
                    else:
                        pe.wait_ge(h2_ready, t if t == 1 else t - 1)
                else:
                    pe.wait_ge(exp_ready, 8 * (NG - 1) if WO_BANKS[t] < 2 else 8 * NG)
                for c in range(PAIRS):
                    hi, lo = oT_hi[:, c, s:s + n], oT_lo[:, c, s:s + n]
                    for k, (x, w) in enumerate(((hi, wo_hi), (hi, wo_lo), (lo, wo_hi))):
                        last = mm(bank[WO_BANKS[t]][0:n, 0:D], x, w[:, c, :],
                                  start=c == 0 and k == 0, stop=c == PAIRS - 1 and k == 2)
                last.then_inc(wo_mm, 1)

            def route(t):
                s, n = TILES[t]
                pe.wait_ge(lnT_ready, t + 1)
                if ROUTER_BANKS[t] == 2:
                    pe.wait_ge(exp_ready, 8 * NG)
                elif ROUTER_BANKS[t] == 3:
                    pe.wait_ge(h2_ready, 5)
                elif t == 0:
                    pe.wait_ge(eT_ready, 2 * NG)
                else:
                    pe.wait_ge(slot_ready, t - 1)
                dst = bank[ROUTER_BANKS[t]][0:n, LOGIT_COLS]
                for c in range(DC):
                    mm(dst, lnT_sb[:, c, s:s + n], rw_sb[:, c, :], start=c == 0, stop=False)
                mm(dst, ones[0:1, 0:n], rb_sb[:, :], start=False, stop=True).then_inc(router_mm, 1)

            def count(t):
                n = TILES[t][1]
                pe.wait_ge(logits_ready, t + 1)
                dst = bank[ROUTER_BANKS[t]][0:n, COUNT_COLS]
                if t:
                    pe.wait_ge(upto_ready, t)
                    mm(dst, ones_bf[:, 0:n], chosen_upto[:, t - 1, :], start=True, stop=False)
                mm(dst, upto_bf[0:n, 0:n], chosen[0:n, t, :], start=t == 0, stop=True).then_inc(count_mm, 1)

            def dispatch(t):
                n = TILES[t][1]
                pe.wait_ge(p_ready, t + 1)
                pe.wait_ge(x_lo_ready, t + 1)
                for c in range(DC):
                    for half in range(2):
                        for part in (x_hi, x_lo):
                            last = mm(bank[XE_BANKS[c][half]][:, 0:HALF_SLOTS], part[0:n, t, c * 128:(c + 1) * 128],
                                      p_sb[0:n, t, 4 * half:4 * half + 4, :].rearrange("p e c -> p (e c)"),
                                      start=t == 0 and part is x_hi, stop=t == NT - 1 and part is x_lo)
                last.then_inc(dispatch_mm, 1)

            def transpose_p(t, q):
                n = TILES[t][1]
                pe.wait_ge(p_ready, t + 1)
                if t or q:
                    pe.wait_ge(pT_ready, 2 * t + q)
                for k in range(4):
                    last = pe.transpose(bank[P_BANK][0:CAP, k * 128:k * 128 + n],
                                        p_sb[0:n, t, 4 * q + k, :].bitcast(f32), ident[0:n, 0:n])
                last.then_inc(p_T, 1)

            for step in range(NG):
                if step == 0:
                    project_qk(late_unit(0, 0))
                    pe.wait_ge(bf_ready, 7)
                    pe.wait_ge(v_ready, 2 * len(AT))
                    pe.wait_ge(qk0_ready, len(QK_UNITS) // 2)
                    pe.wait_ge(lnT_lo_ready, NT)
                    pe.wait_ge(wo_lo_ready, WO_PIECES)
                if step == 1:
                    pe.wait_ge(qk0_ready, EARLY)
                if step == len(AT):
                    pe.wait_ge(qk1_ready, len(QK_UNITS) - EARLY)
                scores(step)
                if step:
                    project_qk(late_unit(step, 0))
                if step == WO_STEP:
                    project_out(0)
                if step >= WO_STEP:
                    transpose_e(step - 1)
                    weigh_v(step - 2)
                    continue
                if step >= 2:
                    weigh_v(step - 2)
                project_qk(late_unit(step, 1))
                if step >= 1:
                    transpose_e(step - 1)
                project_qk(late_unit(step, 2))
            project_out(1)
            transpose_e(NG - 1)
            weigh_v(NG - 2)
            transpose_ln(NT)
            pe.wait_ge(router_in, 32)
            project_out(2)
            transpose_ln(NT + 1)
            route(0)
            weigh_v(NG - 1)
            project_out(3)
            transpose_ln(NT + 2)
            route(1)
            count(0)
            project_out(4)
            transpose_ln(NT + 3)
            pe.wait_ge(oT_lo_ready, NG)
            transpose_p(0, 0)
            route(2)
            count(1)
            transpose_p(0, 1)
            route(3)
            transpose_ln(NT + 4)
            pe.wait_ge(slot_ready, 2)
            pe.wait_ge(h2_ready, 4)
            pe.wait_ge(lnT_ready, 3)
            dispatch(0)
            count(2)
            transpose_p(1, 0)
            dispatch(1)
            count(3)
            route(4)
            transpose_p(1, 1)
            dispatch(2)
            transpose_p(2, 0)
            count(4)
            dispatch(3)
            transpose_p(2, 1)
            dispatch(4)
            pe.wait_ge(slot_ready, NT)
            pe.wait_ge(gate_lo_ready, 1)
            for half in range(2):
                for t, (s, n) in enumerate(TILES):
                    last = mm(bank[GATE_BANKS[half]][0:2 * EXPERTS, 0:HALF_SLOTS],
                              gate_parts[0:n, t, :, :].rearrange("p a e -> p (a e)"),
                              p_sb[0:n, t, 4 * half:4 * half + 4, :].rearrange("p e c -> p (e c)"),
                              start=t == 0, stop=t == NT - 1)
            last.then_inc(gate_mm, 1)
            transpose_p(3, 0)

            def up(e):
                pe.wait_ge(expert_in[e], 32)
                if e % 4 == 0:
                    pe.wait_ge(xe0_ready, e // 4 + 1)
                    pe.wait_ge(xe1_ready, 2)
                for q in range(2):
                    if e >= 1:
                        pe.wait_ge(gelu_ready, 8 * (e - 1) + 4 * (q + 1))
                    elif q == 1:
                        pe.wait_ge(gate_rows_ready, 2)
                    for k in range(4):
                        hc = 4 * q + k
                        for c in range(DC):
                            last = mm(bank[UP_BANKS[q]][:, k * CAP:(k + 1) * CAP], w1_sb[e][:, c, hc * 128:(hc + 1) * 128],
                                      xe_sb[:, c, e, :], start=c == 0, stop=c == DC - 1)
                    last.then_inc(up_mm, 1)

            def down(e):
                if e == 1:
                    pe.wait_ge(pT_ready, 2 * NT)
                if e >= 2:
                    pe.wait_ge(y_biased, e - 1)
                for c in range(HC):
                    if c % (HC // 2) == 0:
                        k = c // (HC // 2)
                        pe.wait_ge(hidden_ready, 2 * e + k + 1)
                        pe.wait_ge(w2_lo_ready, 2 * e + k + 1)
                    hi, lo = hidden_hi[:, e % 2, c, :], hidden_lo[:, e % 2, c, :]
                    for k, (x, w) in enumerate(((hi, w2_hi[e % 2]), (hi, w2_lo[e]), (lo, w2_hi[e % 2]))):
                        last = mm(bank[DOWN_BANKS[e % 2]][0:CAP, 0:D], x, w[:, c, :],
                                  start=c == 0 and k == 0, stop=c == HC - 1 and k == 2)
                last.then_inc(down_mm, 1)

            def combine(e):
                pe.wait_ge(y_ready, e + 1)
                if e == 0:
                    pe.wait_ge(xe0_ready, 2)
                for t, (s, n) in enumerate(TILES):
                    for part in (y_hi, y_lo):
                        last = mm(bank[t // 2][0:n, (t % 2) * D:(t % 2 + 1) * D], pT_sb[:, e, s:s + n], part[:, e % 2, :],
                                  start=e == 0 and part is y_hi and t % 2 == 0,
                                  stop=e == EXPERTS - 1 and part is y_lo and (t % 2 == 1 or t == NT - 1),
                                  skip_group_check=True)
                    if e == EXPERTS - 1 and (t % 2 == 1 or t == NT - 1):
                        last.then_inc(y_final, 1)
                if e < EXPERTS - 1:
                    last.then_inc(combine_mm, 1)

            up(0)
            transpose_p(3, 1)
            for e in range(EXPERTS):
                last = pe.transpose(bank[GATE_T_BANK][0:CAP, e * 2 * EXPERTS:(e + 1) * 2 * EXPERTS], gate_rows[:, e, :],
                                    ident[0:2 * EXPERTS, 0:2 * EXPERTS])
            last.then_inc(gate_T, 1)
            up(1)
            transpose_p(4, 0)
            down(0)
            transpose_p(4, 1)
            for e in range(1, EXPERTS):
                if e + 1 < EXPERTS:
                    up(e + 1)
                down(e)
                combine(e - 1)
            combine(EXPERTS - 1)


def constants():
    import numpy as np

    c = np.zeros((128, C_END), np.float32)
    c[:, C_ID:C_ID + 128] = np.eye(128)
    c[:, C_TRI:C_TRI + 128] = np.triu(np.ones((128, 128)))
    c[:, C_ONE:C_ONE + 128] = 1.0
    c[:, C_SLOT:C_SLOT + CAP] = np.arange(1, CAP + 1)
    c[:, C_EXP:C_EXP + EXPERTS] = np.arange(EXPERTS)
    c[:, C_EPS] = EPS
    for i in range(PER):
        mine = slice(i * SEQ, (i + 1) * SEQ)
        for row in (i, 64 + i):
            c[row, C_ML:C_ML + W3][mine] = 1.0
            c[row, C_MR:C_MR + W3] = -BIG
            c[row, C_MR:C_MR + W3][mine] = 0.0
    sel = np.zeros((EMB_ROWS, IMAGES, SEQ), np.float32)
    for i in range(SEQ):
        sel[i, :, i] = 1.0
        sel[SEQ if i else SEQ + 1, :, i] = 1.0
    return c, sel.reshape(EMB_ROWS, TOKENS)


def kernel(x, L0_tok_W, L0_tok_b, L0_tok_class_token, L0_tok_pos_embedding, L0_attn_Wq, L0_attn_bq, L0_attn_Wk,
           L0_attn_bk, L0_attn_Wv, L0_attn_bv, L0_attn_Wo, L0_attn_bo, L0_ffn_router_w, L0_ffn_router_b, L0_ffn_w1,
           L0_ffn_b1, L0_ffn_w2, L0_ffn_b2):
    import numpy as np
    import concourse.bacc as bacc
    from concourse.bass_utils import run_bass_kernel_spmd

    p = np.asarray(x).reshape(IMAGES, CHANNELS, GRID, PATCH, GRID, PATCH).transpose(1, 3, 5, 0, 2, 4)
    cols = np.zeros((PATCH_IN, IMAGES, SEQ), np.float32)
    cols[:, :, 1:] = p.reshape(PATCH_IN, IMAGES, GRID * GRID)
    padded = np.zeros((PATCH_IN, NT * 128), np.float32)
    padded[:, :TOKENS] = cols.reshape(PATCH_IN, TOKENS)
    consts, sel = constants()
    arrays = {
        "patches": padded.reshape(PC, 128, NT, 128).transpose(1, 2, 0, 3),
        "wT": np.asarray(L0_tok_W).T.reshape(PC, 128, D).transpose(1, 0, 2),
        "emb": np.concatenate([np.asarray(L0_tok_pos_embedding)[0], np.asarray(L0_tok_b)[None],
                               np.asarray(L0_tok_class_token)[0]]),
        "emb_sel": sel, "consts": consts,
        "wq": L0_attn_Wq, "wk": L0_attn_Wk, "wv": L0_attn_Wv,
        "bqk": np.stack([np.asarray(L0_attn_bq), np.asarray(L0_attn_bk)]).reshape(2, PAIRS, 128).transpose(2, 0, 1),
        "bv": L0_attn_bv, "wo": L0_attn_Wo, "bo": L0_attn_bo, "rw": L0_ffn_router_w, "rb": L0_ffn_router_b,
        "w1": L0_ffn_w1, "b1": np.asarray(L0_ffn_b1).reshape(EXPERTS, HC, 128).transpose(2, 0, 1),
        "w2": L0_ffn_w2, "b2": L0_ffn_b2,
    }
    arrays = {k: np.ascontiguousarray(v) for k, v in arrays.items()}
    nc = bacc.Bacc("TRN2", target_bir_lowering=False, num_devices=1)
    args = [nc.dram_tensor(k, a.shape, mybir.dt.from_np(a.dtype), kind="ExternalInput").ap() for k, a in arrays.items()]
    out = nc.dram_tensor("out", (TOKENS, D), mybir.dt.float32, kind="ExternalOutput").ap()
    build(nc, *args, out)
    r = run_bass_kernel_spmd(nc, [arrays], core_ids=[0])
    return r.results[0]["out"].reshape(IMAGES, SEQ, D)
```
